# Optimizing a Trainium2 kernel written in Bass

```python
import numpy as np
import jax
import jax.numpy as jnp

def _softmax(x, axis=-1):
    return jax.nn.softmax(x, axis=axis)

def _gelu(x):
    return jax.nn.gelu(x, approximate=True)

def _silu(x):
    return jax.nn.silu(x)

def _sigmoid(x):
    return jax.nn.sigmoid(x)

def _layernorm(x, axis=-1, eps=1e-05):
    m = jnp.mean(x, axis=axis, keepdims=True)
    v = jnp.var(x, axis=axis, keepdims=True)
    return (x - m) / jnp.sqrt(v + eps)

def _scatter_add(tgt, idx, src, axis=0):
    return tgt.at[idx].add(src)

def _segment_sum(src, seg, n):
    return jax.ops.segment_sum(src, seg, n)
kernel_name = 'mk_gnn_preln_d2_gnn_r64_a6bd6e'

def setup_inputs(seed: int=0):
    np.random.seed(seed)
    _w = jnp.asarray

    def _rec_inputs():
        import jax
        import jax.numpy as jnp
        _gk = jax.random.key(seed)
        x = -0.000202 + 1 * jax.random.normal(jax.random.fold_in(_gk, 1), (100000, 128), jnp.float32)
        src = jax.random.randint(jax.random.fold_in(_gk, 2), (25000,), 0, 100000, jnp.int32)
        dst = jnp.minimum((100000 * jax.random.uniform(jax.random.fold_in(_gk, 3), (25000,)) ** 2.0).astype(jnp.int32), 99999)
        _o = jnp.argsort(dst, stable=True)
        src = src[_o]
        dst = dst[_o]
        edge_attr_64 = 0.000102155 + 1.00015 * jax.random.normal(jax.random.fold_in(_gk, 11), (25000, 64), jnp.float32)
        edge_weight = jax.random.uniform(jax.random.fold_in(_gk, 13), (25000,), jnp.float32, 0.0, 0.999999)
        return (x, src, dst, edge_attr_64, edge_weight)
    x, src, dst, edge_attr_64, edge_weight = _rec_inputs()

    def _L0_gnn_setup():
        import jax, jax.numpy as jnp
        import numpy as np
        N_NODES = 50000
        N_EDGES = 12500
        F_IN = 128
        HEADS = 8
        C = 16
        NEG_SLOPE = 0.2
        key = jax.random.key(seed)
        k1, k2, k3, k4, k5, k6 = jax.random.split(key, 6)
        x = jax.random.normal(k1, (N_NODES, F_IN), dtype=jnp.float32)
        edge_index = jax.random.randint(k2, (2, N_EDGES), 0, N_NODES, dtype=jnp.int32)
        s = 1.0 / np.sqrt(F_IN)
        W_l = jax.random.normal(k3, (HEADS * C, F_IN), dtype=jnp.float32) * s
        W_r = jax.random.normal(k4, (HEADS * C, F_IN), dtype=jnp.float32) * s
        att = jax.random.normal(k5, (HEADS, C), dtype=jnp.float32) * s
        bias = jax.random.normal(k6, (HEADS * C,), dtype=jnp.float32) * 0.01
        return {'x': x, 'edge_index': edge_index, 'W_l': W_l, 'W_r': W_r, 'att': att, 'bias': bias}
    _L0_gnn_all = _L0_gnn_setup()
    _L0_gnn_in = {k: v for k, v in _L0_gnn_all.items() if k in ('W_l', 'W_r', 'att', 'bias')}
    del _L0_gnn_all

    def _L1_gnn_setup():
        import jax, jax.numpy as jnp
        import numpy as np
        N_NODES = 100000
        N_EDGES = 500000
        IN_CH = 128
        EDGE_CH = 64

        def _glorot(key, shape):
            fan_in, fan_out = (shape[0], shape[1])
            lim = (6.0 / (fan_in + fan_out)) ** 0.5
            return jax.random.uniform(key, shape, jnp.float32, -lim, lim)
        key = jax.random.key(seed)
        ks = jax.random.split(key, 14)
        x = jax.random.normal(ks[0], (N_NODES, IN_CH), jnp.float32)
        edge_index = jax.random.randint(ks[1], (2, N_EDGES), 0, N_NODES, jnp.int64)
        edge_attr = jax.random.normal(ks[2], (N_EDGES, EDGE_CH), jnp.float32)
        timestamps = jax.random.uniform(ks[3], (N_EDGES,), jnp.float32)
        We1 = _glorot(ks[4], (EDGE_CH, 2 * EDGE_CH))
        be1 = jnp.zeros((2 * EDGE_CH,), jnp.float32)
        We2 = _glorot(ks[5], (2 * EDGE_CH, IN_CH))
        be2 = jnp.zeros((IN_CH,), jnp.float32)
        Wt = _glorot(ks[6], (1, IN_CH))
        bt = jnp.zeros((IN_CH,), jnp.float32)
        Wn1 = _glorot(ks[7], (2 * IN_CH, IN_CH))
        bn1 = jnp.zeros((IN_CH,), jnp.float32)
        Wn2 = _glorot(ks[8], (IN_CH, IN_CH))
        bn2 = jnp.zeros((IN_CH,), jnp.float32)
        return {'x': x, 'edge_index': edge_index, 'edge_attr': edge_attr, 'timestamps': timestamps, 'We1': We1, 'be1': be1, 'We2': We2, 'be2': be2, 'Wt': Wt, 'bt': bt, 'Wn1': Wn1, 'bn1': bn1, 'Wn2': Wn2, 'bn2': bn2}
    _L1_gnn_all = _L1_gnn_setup()
    _L1_gnn_in = {k: v for k, v in _L1_gnn_all.items() if k in ('We1', 'be1', 'We2', 'be2', 'Wt', 'bt', 'Wn1', 'bn1', 'Wn2', 'bn2')}
    del _L1_gnn_all
    return {'x': x, 'src': src, 'dst': dst, 'edge_attr_64': edge_attr_64, 'edge_weight': edge_weight, 'L0_gnn_W_l': _L0_gnn_in['W_l'], 'L0_gnn_W_r': _L0_gnn_in['W_r'], 'L0_gnn_att': _L0_gnn_in['att'], 'L0_gnn_bias': _L0_gnn_in['bias'], 'L1_gnn_We1': _L1_gnn_in['We1'], 'L1_gnn_be1': _L1_gnn_in['be1'], 'L1_gnn_We2': _L1_gnn_in['We2'], 'L1_gnn_be2': _L1_gnn_in['be2'], 'L1_gnn_Wt': _L1_gnn_in['Wt'], 'L1_gnn_bt': _L1_gnn_in['bt'], 'L1_gnn_Wn1': _L1_gnn_in['Wn1'], 'L1_gnn_bn1': _L1_gnn_in['bn1'], 'L1_gnn_Wn2': _L1_gnn_in['Wn2'], 'L1_gnn_bn2': _L1_gnn_in['bn2']}

def reference(x, src, dst, edge_attr_64, edge_weight, L0_gnn_W_l, L0_gnn_W_r, L0_gnn_att, L0_gnn_bias, L1_gnn_We1, L1_gnn_be1, L1_gnn_We2, L1_gnn_be2, L1_gnn_Wt, L1_gnn_bt, L1_gnn_Wn1, L1_gnn_bn1, L1_gnn_Wn2, L1_gnn_bn2):
    import jax
    import jax.numpy as jnp

    def _L0_gnn_ref(x, edge_index, W_l, W_r, att, bias):
        import jax, jax.numpy as jnp
        import numpy as np
        N_NODES = 50000
        N_EDGES = 12500
        F_IN = 128
        HEADS = 8
        C = 16
        NEG_SLOPE = 0.2
        n = x.shape[0]
        src, dst = (edge_index[0], edge_index[1])
        x_l = (x @ W_l.T).reshape(n, HEADS, C)
        x_r = (x @ W_r.T).reshape(n, HEADS, C)
        x_j = x_l[src]
        x_i = x_r[dst]
        e = jax.nn.leaky_relu(x_i + x_j, NEG_SLOPE)
        alpha = jnp.einsum('mhc,hc->mh', e, att)
        amax = jax.ops.segment_max(alpha, dst, num_segments=n)
        ea = jnp.exp(alpha - amax[dst])
        denom = jax.ops.segment_sum(ea, dst, num_segments=n)
        alpha = ea / (denom[dst] + 1e-16)
        out = jax.ops.segment_sum(x_j * alpha[..., None], dst, num_segments=n)
        out = out.reshape(n, HEADS * C) + bias
        return out

    def _L1_gnn_ref(x, edge_index, edge_attr, timestamps, We1, be1, We2, be2, Wt, bt, Wn1, bn1, Wn2, bn2):
        import jax, jax.numpy as jnp
        import numpy as np
        N_NODES = 100000
        N_EDGES = 500000
        IN_CH = 128
        EDGE_CH = 64

        def _glorot(key, shape):
            fan_in, fan_out = (shape[0], shape[1])
            lim = (6.0 / (fan_in + fan_out)) ** 0.5
            return jax.random.uniform(key, shape, jnp.float32, -lim, lim)
        ts = timestamps[:, None]
        ef = jax.nn.relu(edge_attr @ We1 + be1) @ We2 + be2
        tw = jax.nn.sigmoid(ts @ Wt + bt)
        ef = ef * tw
        row, col = (edge_index[0], edge_index[1])
        combined = jnp.concatenate([x[row], ef], axis=1)
        msg = jax.nn.relu(combined @ Wn1 + bn1) @ Wn2 + bn2
        out = jax.ops.segment_sum(msg, col, num_segments=x.shape[0])
        return out + x
    edge_index = jnp.stack([src, dst])
    h = jnp.maximum(_layernorm(x, axis=-1), 0.0)
    x = x + _L0_gnn_ref(h, edge_index, L0_gnn_W_l, L0_gnn_W_r, L0_gnn_att, L0_gnn_bias)
    h = jnp.maximum(_layernorm(x, axis=-1), 0.0)
    x = x + _L1_gnn_ref(h, edge_index, edge_attr_64, edge_weight, L1_gnn_We1, L1_gnn_be1, L1_gnn_We2, L1_gnn_be2, L1_gnn_Wt, L1_gnn_bt, L1_gnn_Wn1, L1_gnn_bn1, L1_gnn_Wn2, L1_gnn_bn2)
    return x

_drawn_inputs = setup_inputs


def setup_inputs(seed=0):
    import zlib

    import numpy as np

    out = dict(_drawn_inputs(seed))
    spreads = {'L1_gnn_be1': (0.0, 0.8),
     'L1_gnn_be2': (0.0, 0.783),
     'L1_gnn_bt': (0.0, 2.0),
     'L1_gnn_bn1': (0.0, 0.298),
     'L1_gnn_bn2': (0.0, 0.1)}
    factors = {'edge_weight': 8.0,
     'L0_gnn_W_r': 8.0,
     'L0_gnn_att': 8.0,
     'L0_gnn_bias': 4.998,
     'L1_gnn_Wt': 8.0}
    for name, (base, spread) in spreads.items():
        noise = np.random.default_rng([zlib.crc32(name.encode()), seed]).standard_normal(out[name].shape)
        drawn = base * np.exp(spread * noise) if base else spread * noise
        out[name] = jnp.asarray(drawn.astype(out[name].dtype))
    for name, factor in factors.items():
        out[name] = (out[name] * factor).astype(out[name].dtype)
    return out
```

```python
from contextlib import ExitStack

import concourse.bass as bass
from concourse import mybir

F32 = mybir.dt.float32
BF16 = mybir.dt.bfloat16
I32 = mybir.dt.int32
ALU = mybir.AluOpType
ACT = mybir.ActivationFunctionType

P = 128
TILES = 4
GE = TILES * P
EPS = 1e-5
BIG = float(2 ** 100)
NOWHERE = 2 ** 17
ROWS = 16
AHEAD, BEHIND = 2, 2


def known(r):
    return isinstance(r, int)


def live(r, c, count):
    return not known(r) or 0 <= 4 * r + c < count


def later(r, c, d):
    return not known(r) or 4 * r + c >= d


def run_steps(eng, step, count):
    turns = (count - AHEAD) // 4 - 1
    for c in range(-AHEAD, 4):
        step(0, c)
    with eng.Fori(1, 1 + turns) as r:
        for c in range(4):
            step(r, c)
    for c in range(4 * (1 + turns), count + BEHIND):
        step(0, c)


def gnn_program(nc, x, src, dst, edge_attr, edge_weight, W_l, W_r, att, bias0,
                We1, be1, We2, be2, Wt, bt, Wn1, bn1, Wn2, bn2, out):
    N, D = x.shape
    E = src.shape[0]
    EC = edge_attr.shape[1]
    H, C = att.shape
    NT = -(-E // P)
    NG = -(-NT // TILES)
    assert D == P and H * C == P and NT == NG * TILES and 2 * P >= NT > P
    TA, TB = P, NT - P
    FULL_B, REST = E // P - P, E % P
    CH = P * ROWS
    NC = -(-N // CH)
    assert NC == NG and NG >= 12
    x_tab = nc.dram_tensor("x1_table", (N, D), F32).ap()
    keep_d = nc.dram_tensor("keep_flags", (NT * P,), BF16).ap()
    cap_d = nc.dram_tensor("max_caps", (NT * P,), BF16).ap()

    with ExitStack() as ctx:
        def sb(name, shape, dt=F32):
            return ctx.enter_context(nc.sbuf_tensor(name, shape, dt))

        def ps(name, shape):
            return ctx.enter_context(nc.psum_tensor(name, shape, F32))

        def sem(name):
            return ctx.enter_context(nc.semaphore(name))

        def sems(name, n):
            return [sem(f"{name}{i}") for i in range(n)]

        ident = sb("ident", [P, P])
        att_mix = sb("att_mix", [P, P])
        att_col = sb("att_col", [P, 1])
        wl_rows = sb("wl_rows", [P, P])
        wr_rows = sb("wr_rows", [P, P])
        wlT = sb("wlT", [P, P])
        wrT = sb("wrT", [P, P])
        bias_all = sb("bias_all", [P, P])
        eps_col = sb("eps_col", [P, 1])
        we1 = sb("we1", [EC, P])
        we2 = sb("we2", [P, P])
        wt_row = sb("wt_row", [1, P])
        wn1a = sb("wn1a", [P, P])
        wn1b = sb("wn1b", [P, P])
        wn2 = sb("wn2", [P, P])
        cols = sb("cols", [P, 5])
        half = sb("half", [P, 2])
        rows_i = sb("rows_i", [P, 5, 2, P], I32)
        rows_f = sb("rows_f", [P, 3, 2, P])
        keep_r = sb("keep_r", [P, 2, P])
        flag_r = sb("flag_r", [P, 2, 2, P], BF16)
        table = sb("table", [P, NG, 3, TILES], I32)
        idx = sb("idx", [P, 4, 3, TILES], I32)
        x1 = sb("x1", [P, NG, GE])
        xg = sb("xg", [P, 4, 2, GE])
        stat = sb("stat", [P, 2, 16, 6])
        mean2 = sb("mean2", [P, 2, 16])
        dmean = sb("dmean", [P, 2, 16])
        m2 = sb("m2", [P, 2, 16])
        var = sb("var", [P, 2, 16])
        lnv = sb("lnv", [P, 16])
        rstd = sb("rstd", [P, 2, 16])
        nmr = sb("nmr", [P, 2, 16])
        xc = sb("xc", [P, 2, ROWS * P])
        xn = xc[:, 0].rearrange("p (b s e) -> p b s e", b=2, s=2)
        hT = xc[:, 1].rearrange("p (b s e) -> p b s e", b=2, s=2)
        xsum = sb("xsum", [P, GE])
        lk = sb("lk", [P, GE])
        cap = sb("cap", [P, 4, GE], BF16)
        carry = sb("carry", [P, 1])
        mc = sb("mc", [P, GE])
        delta = sb("delta", [P, GE])
        dd = sb("dd", [P, 2, GE])
        pp = sb("pp", [P, 2, GE])
        px = sb("px", [P, GE])
        accT = sb("accT", [P, 2, GE])
        denT = sb("denT", [P, 2, GE])
        rden = sb("rden", [P, TILES * H])
        attn = sb("attn", [P, GE])
        yc = sb("yc", [P, 2, ROWS * P])
        ew = sb("ew", [1, 4, GE])
        ea = rows_i[:, 0:4].rearrange("p b s (t d) -> p b (s t) d", d=EC).bitcast(F32)

        psT = ps("psT", [P, 2, GE])
        psL = ps("psL", [P, 2, GE])
        psS = ps("psS", [P, GE])
        psA = ps("psA", [P, GE])
        psO = ps("psO", [P, GE])
        psD = ps("psD", [P, GE])

        block = ctx.enter_context(nc.Block())

        s_pool_go = sem("pool_goes_on")
        s_sp_go = sem("sp_goes_on")
        s_load = sem("weights_in")
        s_pad = sem("pads_set")
        s_rows = sem("edge_rows_in")
        s_const = sem("constants_set")
        s_ident = sem("ident_set")
        s_mix = sem("att_mix_set")
        s_zero = sem("carry_set")
        s_fl = sem("flags_made")
        s_flag_out = sem("flags_out")
        s_setT = sem("setup_transposed")
        s_table = sem("table_ready")
        idx_in = sems("idx_in", 4)
        cap_in = sems("cap_in", 4)
        copied = sems("table_copied", 2)
        got = sems("rows_gathered", 4)
        s_stat = sem("stats_done")
        s_var = sem("var_done")
        s_rstd = sem("rstd_done")
        s_ln = sem("ln_done")
        s_nmr = sem("nmr_done")
        s_xn = sem("norm_done")
        s_T = sem("h_turned")
        s_hT = sem("h_copied")
        s_S = sem("products_done")
        s_xs = sem("sum_copied")
        s_lk = sem("leaky_done")
        s_A = sem("scores_done")
        s_mc = sem("max_steps")
        s_dd = sem("exponents_done")
        s_pp = sem("exp_done")
        s_px = sem("weighted_done")
        s_acc = sem("sums_done")
        s_O = sem("sums_turned")
        s_rd = sem("den_steps")
        s_att = sem("attention_rows")
        s_x1 = sem("x1_done")
        idx2_in = sems("idx2_in", 4)
        chunk_in = sems("chunk_in", 2)
        s_xb = sem("chunk_biased")
        s_stat2 = sem("chunk_stats")
        s_var2 = sem("chunk_var")
        s_ln2 = sem("chunk_ln")
        s_rstd2 = sem("chunk_rstd")
        s_nmr2 = sem("chunk_nmr")
        s_n2 = sem("chunk_norm")
        s_y2 = sem("chunk_done")
        chunk_out = sems("chunk_out", 2)
        s_stage = sem("x1_staged")
        x1_out = sems("x1_scattered", 4)
        in3 = sems("edges_in", 4)
        got3 = sems("x1_gathered", 4)
        s_xb3 = sem("rows_biased")
        s_stat3 = sem("stats3")
        s_var3 = sem("var3")
        s_ln3 = sem("ln3")
        s_rstd3 = sem("rstd3")
        s_nmr3 = sem("nmr3")
        s_xn3 = sem("norm3")
        s_y0 = sem("y0_done")
        s_T3 = sem("turned3")
        s_hT3 = sem("h2_copied")
        s_m1 = sem("mm_edge1")
        s_h1 = sem("h1_done")
        s_m2 = sem("mm_edge2")
        s_ef = sem("ef_done")
        s_mt = sem("mm_time")
        s_tw = sem("tanh_done")
        s_gt = sem("gated_done")
        s_m3 = sem("mm_node1")
        s_r = sem("r_done")
        s_m4 = sem("mm_node2")
        s_msg = sem("msg_done")
        s_sum = sem("msg_sums")
        s_O3 = sem("msg_turned")
        s_y3 = sem("y_done")
        y_out = sems("y_scattered", 4)

        N_WEIGHTS = 11 + 5 - 1
        keep_rows = keep_d.rearrange("(t e) -> t e", e=P)
        cap_rows = cap_d.rearrange("(t e) -> t e", e=P)

        def uses(r, c):
            return r + c // 4

        def pair_uses(r, c):
            return 2 * r + c // 2

        @block.sync
        def _(sp):
            dma = sp.dma_start
            sp.wait_ge(s_pad, 5)
            for k, (a, shift) in enumerate(((dst, 0), (dst, -1), (dst, 1), (src, 0), (dst, 0))):
                lo = 1 if shift == -1 else 0
                hi = 1 if shift == 1 else 0
                if lo:
                    dma(rows_i[0:1, k, 0, 1:P], a[0:P - 1].rearrange("(a b) -> a b", a=1)).then_inc(s_rows, 16)
                    dma(rows_i[1:P, k, 0, :], a[P - 1:TA * P - 1].rearrange("(a b) -> a b", b=P)).then_inc(s_rows, 16)
                else:
                    dma(rows_i[:, k, 0, :], a[shift:TA * P + shift].rearrange("(a b) -> a b", b=P)).then_inc(s_rows, 16)
                at = TA * P + shift
                dma(rows_i[0:FULL_B, k, 1, :], a[at:at + FULL_B * P].rearrange("(a b) -> a b", b=P)).then_inc(s_rows, 16)
                at += FULL_B * P
                dma(rows_i[FULL_B:FULL_B + 1, k, 1, 0:REST - hi],
                    a[at:at + REST - hi].rearrange("(a b) -> a b", a=1)).then_inc(s_rows, 16)
            for tile, source in ((wl_rows, W_l), (wr_rows, W_r), (we1, We1), (we2, We2),
                                 (wt_row, Wt), (wn1a, Wn1[0:P, :]), (wn1b, Wn1[P:2 * P, :]), (wn2, Wn2),
                                 (att_col, att.rearrange("h (c a) -> (h c) a", a=1)),
                                 (bias_all, bias0.rearrange("(a d) -> a d", a=1).to_broadcast([P, P]))):
                dma(tile[:, :], source).then_inc(s_load, 16)
            for k, source in enumerate((be1, be2, bt, bn1, bn2)):
                dma(cols[:, k:k + 1], source.rearrange("(d a) -> d a", a=1)).then_inc(s_load, 16)
            sp.wait_ge(s_fl, 4)
            for k, d in enumerate((keep_rows, cap_rows)):
                dma(d[0:TA, :], flag_r[:, k, 0, :]).then_inc(s_flag_out, 16)
                dma(d[TA:NT, :], flag_r[0:TB, k, 1, :]).then_inc(s_flag_out, 16)
            sp.wait_ge(s_flag_out, 64)
            sp.wait_ge(s_table, 2)

            def copy_chunk(r, c):
                at = r * (4 * CH) + c * CH if not (known(r) and 4 * r + c == NC - 1) else N - CH
                if later(r, c, 2):
                    sp.wait_ge(copied[c % 2], 16 * pair_uses(r, c))
                if known(r) and 4 * r + c == NC - 1:
                    sp.wait_ge(copied[(c - 1) % 2], 16 * (pair_uses(r, c - 1) + 1))
                dma(x_tab[bass.ds(at, CH), :].rearrange("(p k) d -> p (k d)", p=P),
                    x[bass.ds(at, CH), :].rearrange("(p k) d -> p (k d)", p=P)).then_inc(copied[c % 2], 16)

            def phase1(r, c):
                c += 2
                if live(r, c, NG):
                    b = c % 4
                    if later(r, c, 4):
                        sp.wait_ge(got[b], 16 * 2 * TILES * uses(r, c))
                    sp.sem_inc(s_sp_go, 1)
                    dma(idx[:, b], table[:, bass.ds(r * 4 + c, 1)].rearrange("p a k t -> p (a k) t")).then_inc(idx_in[b], 16)
                    if later(r, c, 4):
                        sp.wait_ge(s_dd, r * 4 + c - 3)
                    dma(cap[:, b], cap_d[bass.ds(r * 4 * GE + c * GE, GE)].rearrange("(a e) -> a e", a=1)
                        .to_broadcast([P, GE])).then_inc(cap_in[b], 16)
                    copy_chunk(r, c)

            run_steps(sp, phase1, NG)

            def chunk_rows(tensor, r, c):
                at = N - CH if known(r) and 4 * r + c == NC - 1 else r * (4 * CH) + c * CH
                return tensor[bass.ds(at, CH), :].rearrange("(p k) d -> p (k d)", p=P)

            sp.wait_ge(s_x1, NG)

            def phase2(r, c):
                if live(r, c + 1, NG):
                    g = c + 1
                    if later(r, g, 2):
                        sp.wait_ge(s_y2, r * 4 + g - 1)
                    dma(xc[:, g % 2], chunk_rows(x, r, g)).then_inc(chunk_in[g % 2], 16)
                    b = g % 4
                    if later(r, g, 4):
                        sp.wait_ge(x1_out[b], 16 * TILES * uses(r, g))
                    else:
                        sp.wait_ge(got[b], 16 * 2 * TILES * ((NG - 1 - b) // 4 + 1))
                    sp.sem_inc(s_sp_go, 1)
                    dma(idx[:, b], table[:, bass.ds(r * 4 + g, 1)].rearrange("p a k t -> p (a k) t")).then_inc(idx2_in[b], 16)
                g = c - 1
                if live(r, g, NC):
                    sp.wait_ge(s_y2, r * 4 + g + 1)
                    if known(r) and 4 * r + g == NC - 1:
                        sp.wait_ge(chunk_out[(g - 1) % 2], 16 * (pair_uses(r, g - 1) + 1))
                    dma(chunk_rows(out, r, g), yc[:, g % 2]).then_inc(chunk_out[g % 2], 16)

            run_steps(sp, phase2, NG)

            def phase3(r, c):
                c += 2
                if live(r, c, NG):
                    b = c % 4
                    if later(r, c, 4):
                        sp.wait_ge(y_out[b], 16 * TILES * uses(r, c))
                        sp.sem_inc(s_sp_go, 1)
                        sp.wait_ge(s_sum, r * 4 + c - 3)
                    else:
                        sp.wait_ge(x1_out[b], 16 * TILES * ((NG - 1 - b) // 4 + 1))
                    sp.sem_inc(s_sp_go, 1)
                    dma(idx[:, b], table[:, bass.ds(r * 4 + c, 1)].rearrange("p a k t -> p (a k) t")).then_inc(in3[b], 16)
                    dma(cap[:, b], keep_d[bass.ds(r * 4 * GE + c * GE, GE)].rearrange("(a e) -> a e", a=1)
                        .to_broadcast([P, GE])).then_inc(in3[b], 16)
                    if known(r) and 4 * r + c == NG - 1:
                        at, full = (NG - 1) * GE, (E - (NG - 1) * GE) // P
                        dma(ew[:, b, 0:E - at], edge_weight[at:E].rearrange("(a e) -> a e", a=1)).then_inc(in3[b], 16)
                        dma(ea[:, b, 0:full], edge_attr[at:at + full * P, :].rearrange("(t p) d -> p t d", p=P)).then_inc(in3[b], 16)
                        dma(ea[0:REST, b, full], edge_attr[at + full * P:E, :]).then_inc(in3[b], 16)
                    else:
                        dma(ew[:, b], edge_weight[bass.ds(r * 4 * GE + c * GE, GE)].rearrange("(a e) -> a e", a=1)).then_inc(in3[b], 16)
                        dma(ea[:, b], edge_attr[bass.ds(r * 4 * GE + c * GE, GE), :].rearrange("(t p) d -> p t d", p=P)).then_inc(in3[b], 16)

            run_steps(sp, phase3, NG)
            for b in range(2):
                sp.wait_ge(copied[b], 16 * ((NC - 1 - b) // 2 + 1))
                sp.wait_ge(chunk_out[b], 16 * ((NC - 1 - b) // 2 + 1))
            for b in range(4):
                sp.wait_ge(x1_out[b], 16 * TILES * ((NG - 1 - b) // 4 + 1))
                sp.wait_ge(y_out[b], 16 * TILES * ((NG - 1 - b) // 4 + 1))

        def arrived3(r, c):
            per = 16 * 4
            return per * (uses(r, c) + 1) + (16 if known(r) and 4 * r + c == NG - 1 else 0)

        @block.gpsimd
        def _(pool):
            for k, v in enumerate((0, -1, -1, 0, NOWHERE)):
                pool.memset(rows_i[:, k], v).then_inc(s_pad, 1)
            pool.memset(ident[:, :], 0.0).then_inc(s_const, 1)
            pool.memset(att_mix[:, :], 1.0).then_inc(s_const, 1)
            pool.wait_ge(s_const, 2)
            pool.affine_select(out=ident[:, :], in_=ident[:, :], compare_op=ALU.not_equal, fill=1.0,
                               base=0, pattern=[[-1, P]], channel_multiplier=1).then_inc(s_ident, 1)
            heads = att_mix[:, :].rearrange("p (h c) -> p h c", c=C)
            pool.affine_select(out=heads, in_=heads, compare_op=ALU.is_ge, fill=0.0,
                               base=0, pattern=[[-C, H], [0, C]], channel_multiplier=1).then_inc(s_mix, 1)
            pool.wait_ge(s_mix, 1)
            pool.affine_select(out=heads, in_=heads, compare_op=ALU.is_ge, fill=0.0,
                               base=C - 1, pattern=[[C, H], [0, C]], channel_multiplier=-1).then_inc(s_mix, 1)

            def phase1(r, c):
                c += 2
                if live(r, c, NG):
                    b = c % 4
                    pool.wait_ge(idx_in[b], 16 * (uses(r, c) + 1))
                    if later(r, c, 4):
                        pool.wait_ge(s_x1, r * 4 + c - 3)
                    pool.sem_inc(s_pool_go, 1)
                    for j in range(TILES):
                        for side in range(2):
                            pool.indirect_dma_start(
                                out=xg[:, b, side, j * P:(j + 1) * P], out_offset=None, in_=x,
                                in_offset=bass.IndirectOffsetOnAxis(ap=idx[:, b, side, j:j + 1], axis=0)
                            ).then_inc(got[b], 16)

            pool.wait_ge(s_table, 2)
            run_steps(pool, phase1, NG)

            for b in range(2):
                pool.wait_ge(copied[b], 16 * ((NC - 1 - b) // 2 + 1))

            def phase2(r, c):
                if live(r, c, NG):
                    b = c % 4
                    pool.wait_ge(idx2_in[b], 16 * (uses(r, c) + 1))
                    pool.wait_ge(s_stage, r * 4 + c + 1)
                    pool.sem_inc(s_pool_go, 1)
                    for j in range(TILES):
                        pool.indirect_dma_start(
                            out=x_tab, out_offset=bass.IndirectOffsetOnAxis(ap=idx[:, b, 2, j:j + 1], axis=0),
                            in_=xg[:, b, 1, j * P:(j + 1) * P], in_offset=None,
                            bounds_check=N - 1, oob_is_err=False).then_inc(x1_out[b], 16)

            run_steps(pool, phase2, NG)

            for b in range(4):
                pool.wait_ge(x1_out[b], 16 * TILES * ((NG - 1 - b) // 4 + 1))

            def phase3(r, c):
                g = c + 2
                if live(r, g, NG):
                    b = g % 4
                    pool.wait_ge(in3[b], arrived3(r, g))
                    if later(r, g, 4):
                        pool.wait_ge(s_xn3, r * 4 + g - 3)
                    pool.sem_inc(s_pool_go, 1)
                    for j in range(TILES):
                        pool.indirect_dma_start(
                            out=xg[:, b, 0, j * P:(j + 1) * P], out_offset=None, in_=x_tab,
                            in_offset=bass.IndirectOffsetOnAxis(ap=idx[:, b, 0, j:j + 1], axis=0)
                        ).then_inc(got3[b], 16)
                g = c - 1
                if live(r, g, NG):
                    b = g % 4
                    if known(r) and 4 * r + g == 0:
                        for k in range(2):
                            pool.wait_ge(chunk_out[k], 16 * ((NC - 1 - k) // 2 + 1))
                    pool.wait_ge(s_y3, r * 4 + g + 1)
                    pool.sem_inc(s_pool_go, 1)
                    for j in range(TILES):
                        pool.indirect_dma_start(
                            out=out, out_offset=bass.IndirectOffsetOnAxis(ap=idx[:, b, 2, j:j + 1], axis=0),
                            in_=xg[:, b, 1, j * P:(j + 1) * P], in_offset=None,
                            bounds_check=N - 1, oob_is_err=False).then_inc(y_out[b], 16)

            run_steps(pool, phase3, NG)

        def layernorm_stats(dve, rows, n, b, s_stats, s_variance, g):
            for j in range(n):
                last = dve.bn_stats(stat[:, b, j, :], rows(j))
            last.then_inc(s_stats, 1)
            dve.wait_ge(s_stats, 3 * g + 1)
            dve.tensor_tensor(dmean[:, b, 0:n], stat[:, b, 0:n, 1], stat[:, b, 0:n, 4], ALU.subtract)
            dve.tensor_tensor(m2[:, b, 0:n], stat[:, b, 0:n, 2], stat[:, b, 0:n, 5], ALU.add)
            dve.tensor_tensor(mean2[:, b, 0:n], stat[:, b, 0:n, 1], stat[:, b, 0:n, 4], ALU.add).then_inc(s_stats, 1)
            dve.wait_ge(s_stats, 3 * g + 2)
            dve.tensor_tensor(dmean[:, b, 0:n], dmean[:, b, 0:n], dmean[:, b, 0:n], ALU.mult).then_inc(s_stats, 1)
            dve.wait_ge(s_stats, 3 * g + 3)
            dve.scalar_tensor_tensor(out=var[:, b, 0:n], in0=dmean[:, b, 0:n], scalar=P / 4.0, in1=m2[:, b, 0:n],
                                     op0=ALU.mult, op1=ALU.add).then_inc(s_variance, 1)

        def negative_mean(dve, n, b):
            return dve.scalar_tensor_tensor(out=nmr[:, b, 0:n], in0=mean2[:, b, 0:n], scalar=-0.5,
                                            in1=rstd[:, b, 0:n], op0=ALU.mult, op1=ALU.mult)

        @block.vector
        def _(dve):
            dve.memset(eps_col[:, :], EPS)
            dve.memset(carry[:, :], 0.0).then_inc(s_zero, 1)
            dve.wait_ge(s_rows, 16 * 16)
            dve.tensor_tensor(keep_r[:, :, :], rows_i[:, 0], rows_i[:, 1], ALU.is_equal).then_inc(s_fl, 1)
            dve.tensor_tensor(rows_f[:, 2], rows_i[:, 0], rows_i[:, 2], ALU.is_equal).then_inc(s_fl, 1)
            dve.wait_ge(s_fl, 2)
            dve.tensor_copy(flag_r[:, 0], keep_r[:, :, :]).then_inc(s_fl, 1)
            dve.tensor_scalar(flag_r[:, 1], keep_r[:, :, :], 2 * BIG, -BIG, ALU.mult, ALU.add).then_inc(s_fl, 1)
            dve.tensor_copy(rows_f[:, 0], rows_i[:, 3])
            dve.tensor_copy(rows_f[:, 1], rows_i[:, 0])
            dve.scalar_tensor_tensor(out=rows_f[:, 2], in0=rows_f[:, 2], scalar=float(NOWHERE), in1=rows_i[:, 4],
                                     op0=ALU.mult, op1=ALU.add).then_inc(s_fl, 1)
            dve.wait_ge(s_setT, 1)
            turned = psT[:, :, :].rearrange("p a (k t) -> p (a k) t", t=P)
            for k in range(3):
                dve.tensor_copy(table[:, 0:TA // TILES, k, :],
                                turned[:, k, :].rearrange("p (g t) -> p g t", t=TILES))
            dve.wait_ge(s_setT, 2)
            turned = psL[:, :, :].rearrange("p a (k t) -> p (a k) t", t=P)
            for k in range(3):
                last = dve.tensor_copy(table[:, TA // TILES:NG, k, :],
                                       turned[:, k, 0:TB].rearrange("p (g t) -> p g t", t=TILES))
            last.then_inc(s_table, 1)
            dve.wait_ge(s_setT, 3)
            dve.tensor_copy(wlT[:, :], psS[:, 0:P])
            dve.tensor_copy(wrT[:, :], psS[:, P:2 * P])
            dve.wait_ge(s_load, 16 * N_WEIGHTS)
            dve.wait_ge(s_mix, 2)
            dve.wait_ge(s_zero, 1)
            dve.tensor_scalar(att_mix[:, :], att_mix[:, :], att_col[:, 0:1], None, ALU.mult)
            dve.tensor_scalar(half[:, :], cols[:, 1:3], 0.5, None, ALU.mult).then_inc(s_table, 1)

            def phase1(r, c):
                g = r * 4 + c
                if live(r, c, NG):
                    b = c % 4
                    dve.wait_ge(cap_in[b], 16 * (uses(r, c) + 1))
                    dve.wait_ge(s_A, g + 1)
                    dve.tensor_tensor(mc[:, 0:1], carry[:, :], cap[:, b, 0:1], ALU.min).then_inc(s_mc, 1)
                    dve.wait_ge(s_mc, 3 * g + 1)
                    dve.tensor_tensor_scan(mc[:, 1:GE], psA[:, 0:GE - 1], cap[:, b, 1:GE], mc[:, 0:1],
                                           ALU.max, ALU.min).then_inc(s_mc, 1)
                    dve.wait_ge(s_mc, 3 * g + 2)
                    dve.tensor_tensor(delta[:, :], psA[:, :], mc[:, :], ALU.subtract)
                    dve.tensor_tensor(carry[:, :], psA[:, GE - 1:GE], mc[:, GE - 1:GE], ALU.max).then_inc(s_mc, 1)
                    dve.wait_ge(s_mc, 3 * g + 3)
                    dve.tensor_scalar(dd[:, 0, :], delta[:, :], 0.0, -1.0, ALU.max, ALU.mult)
                    dve.tensor_scalar(dd[:, 1, :], delta[:, :], 0.0, None, ALU.min).then_inc(s_dd, 1)
                if live(r, c + 2, NG):
                    b, h = (c + 2) % 4, c % 2
                    dve.wait_ge(got[b], 16 * 2 * TILES * (uses(r, c + 2) + 1))
                    if later(r, c + 2, 2):
                        dve.wait_ge(s_xn, g + 1)
                    layernorm_stats(dve, lambda j: xg[:, b, j // TILES, (j % TILES) * P:(j % TILES + 1) * P],
                                    2 * TILES, h, s_stat, s_var, g + 2)
                if live(r, c, NG):
                    h = c % 2
                    dve.wait_ge(s_pp, g + 1)
                    dve.tensor_tensor(px[:, :], pp[:, 1, :], psL[:, h, :], ALU.mult).then_inc(s_px, 1)
                if live(r, c + 1, NG):
                    dve.wait_ge(s_xs, g + 2)
                    if later(r, c + 1, 1):
                        dve.wait_ge(s_A, g + 1)
                    dve.scalar_tensor_tensor(out=lk[:, :], in0=xsum[:, :], scalar=0.2, in1=xsum[:, :],
                                             op0=ALU.mult, op1=ALU.max).then_inc(s_lk, 1)
                if live(r, c + 2, NG):
                    h = c % 2
                    dve.wait_ge(s_rstd, g + 3)
                    negative_mean(dve, 2 * TILES, h).then_inc(s_nmr, 1)
                if live(r, c, NG):
                    h = c % 2
                    dve.wait_ge(s_px, g + 1)
                    if later(r, c, 1):
                        dve.wait_ge(s_acc, g)
                    if later(r, c, 2):
                        dve.wait_ge(s_O, g - 1)
                    first = known(r) and r * 4 + c == 0
                    dve.tensor_tensor_scan(accT[:, h, :], pp[:, 0, :], px[:, :],
                                           0.0 if first else accT[:, 1 - h, GE - 1:GE], ALU.mult, ALU.add)
                    dve.tensor_tensor_scan(denT[:, h, :], pp[:, 0, :], pp[:, 1, :],
                                           0.0 if first else denT[:, 1 - h, GE - 1:GE], ALU.mult, ALU.add).then_inc(s_acc, 1)
                g = r * 4 + c - 1
                if live(r, c - 1, NG):
                    b = (c - 1) % 4
                    dve.wait_ge(s_O, g + 1)
                    dve.tensor_scalar(rden[:, :], psD[:, 0:TILES * H], 1e-16, None, ALU.add).then_inc(s_rd, 1)
                    dve.wait_ge(s_rd, 2 * g + 1)
                    dve.reciprocal(rden[:, :], rden[:, :]).then_inc(s_rd, 1)
                    dve.wait_ge(s_rd, 2 * g + 2)
                    dve.tensor_tensor(attn[:, :].rearrange("p (k c) -> p k c", c=C),
                                      psO[:, :].rearrange("p (k c) -> p k c", c=C),
                                      rden[:, :].unsqueeze(2).to_broadcast([P, TILES * H, C]), ALU.mult).then_inc(s_att, 1)
                    dve.wait_ge(s_att, g + 1)
                    dve.tensor_tensor(x1[:, bass.ds(g, 1)].rearrange("p a e -> p (a e)"), attn[:, :], xg[:, b, 1, :], ALU.add).then_inc(s_x1, 1)

            run_steps(dve, phase1, NG)

            def phase2(r, c):
                g, h = r * 4 + c, c % 2
                rows = xc[:, h].rearrange("p (k d) -> p k d", d=D)
                if live(r, c, NC):
                    dve.wait_ge(chunk_in[h], 16 * (pair_uses(r, c) + 1))
                    dve.tensor_tensor(rows, rows, bias_all[:, :].unsqueeze(1).to_broadcast([P, ROWS, D]), ALU.add).then_inc(s_xb, 1)
                    dve.wait_ge(s_xb, g + 1)
                    if later(r, c, 2):
                        dve.wait_ge(s_n2, g - 1)
                    layernorm_stats(dve, lambda j: rows[:, j, :], ROWS, h, s_stat2, s_var2, g)
                if live(r, c - 1, NC):
                    dve.wait_ge(s_n2, g)
                    o = 1 - h
                    dve.tensor_tensor(yc[:, o], yc[:, o], xc[:, o], ALU.add).then_inc(s_y2, 1)
                if live(r, c, NC):
                    dve.wait_ge(s_rstd2, g + 1)
                    negative_mean(dve, ROWS, h).then_inc(s_nmr2, 1)

            run_steps(dve, phase2, NC)

            def phase3(r, c):
                g = r * 4 + c + 1
                if live(r, c + 1, NG):
                    b, h = (c + 1) % 4, (c + 1) % 2
                    dve.wait_ge(got3[b], 16 * TILES * (uses(r, c + 1) + 1))
                    src_rows = xg[:, b, 0, :].rearrange("p (k d) -> p k d", d=D)
                    dst_rows = xg[:, b, 1, :].rearrange("p (k d) -> p k d", d=D)
                    bias_rows = bias_all[:, :].unsqueeze(1).to_broadcast([P, TILES, D])
                    dve.tensor_tensor(src_rows, src_rows, bias_rows, ALU.add)
                    if later(r, c + 1, 4):
                        dve.wait_ge(y_out[b], 16 * TILES * uses(r, c + 1))
                    dve.tensor_tensor(dst_rows, x1[:, bass.ds(g, 1)].rearrange("p a (k d) -> p (a k) d", d=D), bias_rows, ALU.add).then_inc(s_xb3, 1)
                    dve.wait_ge(s_xb3, g + 1)
                    if later(r, c + 1, 2):
                        dve.wait_ge(s_xn3, g - 1)
                    layernorm_stats(dve, lambda j: xg[:, b, j // TILES, (j % TILES) * P:(j % TILES + 1) * P],
                                    2 * TILES, h, s_stat3, s_var3, g)
                g = r * 4 + c
                if live(r, c, NG):
                    b, h = c % 4, c % 2
                    dve.wait_ge(s_xn3, g + 1)
                    dve.tensor_tensor(xg[:, b, 1, :], xg[:, b, 1, :], xn[:, h, 1, :], ALU.add).then_inc(s_y0, 1)
                if live(r, c + 1, NG):
                    h = (c + 1) % 2
                    dve.wait_ge(s_rstd3, g + 2)
                    negative_mean(dve, 2 * TILES, h).then_inc(s_nmr3, 1)
                if live(r, c, NG):
                    dve.wait_ge(s_ef, g + 1)
                    dve.wait_ge(s_tw, g + 1)
                    dve.scalar_tensor_tensor(out=delta[:, :], in0=pp[:, 0, :], scalar=1.0, in1=pp[:, 1, :],
                                             op0=ALU.add, op1=ALU.mult).then_inc(s_gt, 1)
                g = r * 4 + c - 1
                if live(r, c - 1, NG):
                    b = (c - 1) % 4
                    dve.wait_ge(s_O3, g + 1)
                    dve.tensor_tensor(xg[:, b, 1, :], psO[:, :], xg[:, b, 1, :], ALU.add).then_inc(s_y3, 1)
                g = r * 4 + c
                if live(r, c, NG):
                    h, b = c % 2, c % 4
                    dve.wait_ge(s_msg, g + 1)
                    if later(r, c, 1):
                        dve.wait_ge(s_sum, g)
                    if later(r, c, 2):
                        dve.wait_ge(s_O3, g - 1)
                    first = known(r) and r * 4 + c == 0
                    dve.tensor_tensor_scan(accT[:, h, :], cap[:, b, :], px[:, :],
                                           0.0 if first else accT[:, 1 - h, GE - 1:GE], ALU.mult, ALU.add).then_inc(s_sum, 1)

            run_steps(dve, phase3, NG)

        def make_scales(act, n, b, s_variance, s_log, s_scale, g):
            act.wait_ge(s_variance, g + 1)
            act.activation(lnv[:, 0:n], var[:, b, 0:n], ACT.Ln, scale=1.0 / P, bias=eps_col[:, 0:1]).then_inc(s_log, 1)
            act.wait_ge(s_log, g + 1)
            act.activation(rstd[:, b, 0:n], lnv[:, 0:n], ACT.Exp, scale=-0.5).then_inc(s_scale, 1)

        def normalise(act, rows_in, rows_out, n, b):
            for j in range(n):
                last = act.activation(rows_out(j), rows_in(j), ACT.Relu, scale=rstd[:, b, j:j + 1], bias=nmr[:, b, j:j + 1])
            return last

        @block.scalar
        def _(act):
            act.wait_ge(s_table, 2)

            def phase1(r, c):
                g = r * 4 + c + 1
                if live(r, c + 1, NG):
                    h = (c + 1) % 2
                    act.wait_ge(s_T, g + 1)
                    if later(r, c + 1, 2):
                        act.wait_ge(s_S, g - 1)
                    act.copy(hT[:, h], psT[:, :, :]).then_inc(s_hT, 1)
                if live(r, c, NG):
                    act.wait_ge(s_dd, g)
                    act.activation(pp[:, :, :], dd[:, :, :], ACT.Exp).then_inc(s_pp, 1)
                if live(r, c + 1, NG):
                    act.wait_ge(s_S, g + 1)
                    if later(r, c + 1, 1):
                        act.wait_ge(s_lk, g)
                    act.copy(xsum[:, :], psS[:, :]).then_inc(s_xs, 1)
                g = r * 4 + c + 2
                if live(r, c + 2, NG):
                    b, h = (c + 2) % 4, c % 2
                    make_scales(act, 2 * TILES, h, s_var, s_ln, s_rstd, g)
                    act.wait_ge(s_nmr, g + 1)
                    if later(r, c + 2, 2):
                        act.wait_ge(s_T, g - 1)
                    normalise(act, lambda j: xg[:, b, j // TILES, (j % TILES) * P:(j % TILES + 1) * P],
                              lambda j: xn[:, h, j // TILES, (j % TILES) * P:(j % TILES + 1) * P],
                              2 * TILES, h).then_inc(s_xn, 1)

            run_steps(act, phase1, NG)

            act.wait_ge(s_x1, NG)

            def phase2(r, c):
                g, h = r * 4 + c, c % 2
                if live(r, c, NG):
                    b = c % 4
                    if later(r, c, 4):
                        act.wait_ge(x1_out[b], 16 * TILES * uses(r, c))
                    act.copy(xg[:, b, 1, :], x1[:, bass.ds(g, 1)].rearrange("p a e -> p (a e)")).then_inc(s_stage, 1)
                    make_scales(act, ROWS, h, s_var2, s_ln2, s_rstd2, g)
                    act.wait_ge(s_nmr2, g + 1)
                    if later(r, c, 2):
                        act.wait_ge(chunk_out[h], 16 * pair_uses(r, c))
                    rows = xc[:, h].rearrange("p (k d) -> p k d", d=D)
                    normed = yc[:, h].rearrange("p (k d) -> p k d", d=D)
                    normalise(act, lambda j: rows[:, j, :], lambda j: normed[:, j, :], ROWS, h).then_inc(s_n2, 1)

            run_steps(act, phase2, NG)
            act.wait_ge(s_y2, NC)

            def phase3(r, c):
                g = r * 4 + c
                if live(r, c, NG):
                    h = c % 2
                    act.wait_ge(s_T3, g + 1)
                    if later(r, c, 2):
                        act.wait_ge(s_m3, g - 1)
                    act.copy(hT[0:EC, h, 1, :], psT[0:EC, 1, :])
                    act.copy(hT[:, h, 0, :], psT[:, 0, :]).then_inc(s_hT3, 1)
                    act.wait_ge(s_m1, g + 1)
                    act.activation(dd[:, 0, :], psS[:, :], ACT.Relu, bias=cols[:, 0:1]).then_inc(s_h1, 1)
                if live(r, c + 1, NG):
                    make_scales(act, 2 * TILES, (c + 1) % 2, s_var3, s_ln3, s_rstd3, g + 1)
                if live(r, c, NG):
                    act.wait_ge(s_mt, g + 1)
                    if later(r, c, 1):
                        act.wait_ge(s_gt, g)
                    act.activation(pp[:, 0, :], psL[:, 0, :], ACT.Tanh, scale=0.5, bias=half[:, 1:2]).then_inc(s_tw, 1)
                    act.wait_ge(s_m2, g + 1)
                    act.activation(pp[:, 1, :], psA[:, :], ACT.Identity, scale=0.5, bias=half[:, 0:1]).then_inc(s_ef, 1)
                if live(r, c + 1, NG):
                    b, h = (c + 1) % 4, (c + 1) % 2
                    act.wait_ge(s_nmr3, g + 2)
                    if later(r, c + 1, 2):
                        act.wait_ge(s_T3, g)
                        act.wait_ge(s_y0, g)
                    normalise(act, lambda j: xg[:, b, j // TILES, (j % TILES) * P:(j % TILES + 1) * P],
                              lambda j: xn[:, h, j // TILES, (j % TILES) * P:(j % TILES + 1) * P],
                              2 * TILES, h).then_inc(s_xn3, 1)
                if live(r, c, NG):
                    act.wait_ge(s_m3, g + 1)
                    act.activation(dd[:, 1, :], psL[:, 1, :], ACT.Relu, bias=cols[:, 3:4]).then_inc(s_r, 1)
                    act.wait_ge(s_m4, g + 1)
                    if later(r, c, 1):
                        act.wait_ge(s_sum, g)
                    act.activation(px[:, :], psD[:, :], ACT.Identity, bias=cols[:, 4:5]).then_inc(s_msg, 1)
            run_steps(act, phase3, NG)

        @block.tensor
        def _(pe):
            pe.wait_ge(s_ident, 1)
            pe.wait_ge(s_fl, 5)
            for half_, n, to in ((0, TA, psT), (1, TB, psL)):
                for k in range(3):
                    last = pe.transpose(to[:, k // TILES, k * P:k * P + n], rows_f[0:n, k, half_, :], ident[0:n, 0:n])
                last.then_inc(s_setT, 1)
            pe.wait_ge(s_load, 16 * N_WEIGHTS)
            pe.transpose(psS[:, 0:P], wl_rows[:, :], ident[:, :])
            pe.transpose(psS[:, P:2 * P], wr_rows[:, :], ident[:, :]).then_inc(s_setT, 1)
            pe.wait_ge(s_table, 2)

            def phase1(r, c):
                g = r * 4 + c + 1
                if live(r, c + 1, NG):
                    h = (c + 1) % 2
                    pe.wait_ge(s_xn, g + 1)
                    if later(r, c + 1, 1):
                        pe.wait_ge(s_hT, g)
                    for side in range(2):
                        for j in range(TILES):
                            last = pe.transpose(psT[:, side, j * P:(j + 1) * P], xn[:, h, side, j * P:(j + 1) * P], ident[:, :])
                    last.then_inc(s_T, 1)
                g = r * 4 + c - 1
                if live(r, c - 1, NG):
                    h = (c - 1) % 2
                    pe.wait_ge(s_acc, g + 1)
                    if later(r, c - 1, 1):
                        pe.wait_ge(s_att, g)
                    for j in range(TILES):
                        pe.transpose(psO[:, j * P:(j + 1) * P], accT[:, h, j * P:(j + 1) * P], ident[:, :])
                    for j in range(TILES):
                        last = pe.matmul(psD[:, j * H:(j + 1) * H], denT[:, h, j * P:(j + 1) * P], ident[:, 0:P:C],
                                         start=True, stop=True)
                    last.then_inc(s_O, 1)
                g = r * 4 + c + 1
                if live(r, c + 1, NG):
                    h = (c + 1) % 2
                    pe.wait_ge(s_hT, g + 1)
                    if later(r, c + 1, 2):
                        pe.wait_ge(s_px, g - 1)
                    if later(r, c + 1, 1):
                        pe.wait_ge(s_xs, g)
                    pe.matmul(psS[:, :], wlT[:, :], hT[:, h, 0, :], start=True, stop=False)
                    pe.matmul(psS[:, :], wrT[:, :], hT[:, h, 1, :], start=False, stop=True)
                    pe.matmul(psL[:, h, :], wlT[:, :], hT[:, h, 0, :], start=True, stop=True).then_inc(s_S, 1)
                    pe.wait_ge(s_lk, g + 1)
                    if later(r, c + 1, 1):
                        pe.wait_ge(s_dd, g)
                    pe.matmul(psA[:, :], att_mix[:, :], lk[:, :], start=True, stop=True).then_inc(s_A, 1)

            run_steps(pe, phase1, NG)
            pe.wait_ge(s_x1, NG)

            def phase3(r, c):
                g = r * 4 + c
                if live(r, c, NG):
                    b, h = c % 4, c % 2
                    pe.wait_ge(s_xn3, g + 1)
                    pe.wait_ge(in3[b], arrived3(r, c))
                    if later(r, c, 1):
                        pe.wait_ge(s_hT3, g)
                    for j in range(TILES):
                        pe.transpose(psT[:, 0, j * P:(j + 1) * P], xn[:, h, 0, j * P:(j + 1) * P], ident[:, :])
                    for j in range(TILES):
                        last = pe.transpose(psT[0:EC, 1, j * P:(j + 1) * P], ea[:, b, j, :], ident[:, :])
                    last.then_inc(s_T3, 1)
                    if later(r, c, 1):
                        pe.wait_ge(s_tw, g)
                    pe.matmul(psL[:, 0, :], wt_row[:, :], ew[:, b, :], start=True, stop=True).then_inc(s_mt, 1)
                    pe.wait_ge(s_hT3, g + 1)
                    if later(r, c, 1):
                        pe.wait_ge(s_h1, g)
                    pe.matmul(psS[:, :], we1[:, :], hT[0:EC, h, 1, :], start=True, stop=True).then_inc(s_m1, 1)
                if live(r, c - 1, NG):
                    pe.wait_ge(s_sum, g)
                    if later(r, c - 1, 1):
                        pe.wait_ge(s_y3, g - 1)
                    for j in range(TILES):
                        last = pe.transpose(psO[:, j * P:(j + 1) * P], accT[:, (c - 1) % 2, j * P:(j + 1) * P], ident[:, :])
                    last.then_inc(s_O3, 1)
                if live(r, c, NG):
                    h = c % 2
                    pe.wait_ge(s_h1, g + 1)
                    if later(r, c, 1):
                        pe.wait_ge(s_ef, g)
                    pe.matmul(psA[:, :], we2[:, :], dd[:, 0, :], start=True, stop=True).then_inc(s_m2, 1)
                    if later(r, c, 1):
                        pe.wait_ge(s_r, g)
                    pe.matmul(psL[:, 1, :], wn1a[:, :], hT[:, h, 0, :], start=True, stop=False)
                    pe.wait_ge(s_gt, g + 1)
                    pe.matmul(psL[:, 1, :], wn1b[:, :], delta[:, :], start=False, stop=True).then_inc(s_m3, 1)
                    pe.wait_ge(s_r, g + 1)
                    if later(r, c, 1):
                        pe.wait_ge(s_msg, g)
                    pe.matmul(psD[:, :], wn2[:, :], dd[:, 1, :], start=True, stop=True).then_inc(s_m4, 1)

            run_steps(pe, phase3, NG)


_INS = ['x', 'src', 'dst', 'edge_attr_64', 'edge_weight', 'L0_gnn_W_l', 'L0_gnn_W_r', 'L0_gnn_att', 'L0_gnn_bias',
        'L1_gnn_We1', 'L1_gnn_be1', 'L1_gnn_We2', 'L1_gnn_be2', 'L1_gnn_Wt', 'L1_gnn_bt',
        'L1_gnn_Wn1', 'L1_gnn_bn1', 'L1_gnn_Wn2', 'L1_gnn_bn2']


def kernel(**inputs):
    import numpy as _np
    import concourse.bacc as _bacc
    from concourse.bass_utils import run_bass_kernel_spmd as _run

    nc = _bacc.Bacc("TRN2", target_bir_lowering=False, num_devices=1)
    arrays, args = {}, []
    for name in _INS:
        a = _np.ascontiguousarray(inputs[name])
        arrays[f"in_{name}"] = a
        args.append(nc.dram_tensor(f"in_{name}", a.shape, mybir.dt.from_np(a.dtype), kind="ExternalInput").ap())
    out = nc.dram_tensor("out_0", arrays["in_x"].shape, F32, kind="ExternalOutput").ap()
    gnn_program(nc, *args, out)
    r = _run(nc, [arrays], core_ids=[0])
    return r.results[0]["out_0"]
```

```python
from contextlib import ExitStack

import concourse.bass as bass
from concourse import mybir

F32 = mybir.dt.float32
BF16 = mybir.dt.bfloat16
I32 = mybir.dt.int32
ALU = mybir.AluOpType
ACT = mybir.ActivationFunctionType

P = 128
TILES = 4
GE = TILES * P
EPS = 1e-5
NEG_SLOPE = 0.2
BIG = float(2 ** 100)
NOWHERE = 2 ** 17
ROWS = 16
AHEAD, BEHIND = 2, 2


def known(r):
    return isinstance(r, int)


def live(r, c, count):
    return not known(r) or 0 <= 4 * r + c < count


def later(r, c, d):
    return not known(r) or 4 * r + c >= d


def run_steps(eng, step, count):
    turns = (count - AHEAD) // 4 - 1
    for c in range(-AHEAD, 4):
        step(0, c)
    with eng.Fori(1, 1 + turns) as r:
        for c in range(4):
            step(r, c)
    for c in range(4 * (1 + turns), count + BEHIND):
        step(0, c)


def gnn_program(nc, x, src, dst, edge_attr, edge_weight, W_l, W_r, att, bias0,
                We1, be1, We2, be2, Wt, bt, Wn1, bn1, Wn2, bn2, out):
    N, D = x.shape
    E = src.shape[0]
    EC = edge_attr.shape[1]
    H, C = att.shape
    NT = -(-E // P)
    NG = -(-NT // TILES)
    assert D == P and H * C == P and NT == NG * TILES and 2 * P >= NT > P
    TA, TB = P, NT - P
    FULL_B, REST = E // P - P, E % P
    CH = P * ROWS
    NC = -(-N // CH)
    assert NC == NG and NG >= 12
    x_tab = nc.dram_tensor("x1_table", (N, D), F32).ap()
    keep_d = nc.dram_tensor("keep_flags", (NT * P,), BF16).ap()
    cap_d = nc.dram_tensor("max_caps", (NT * P,), BF16).ap()

    with ExitStack() as ctx:
        def sb(name, shape, dt=F32):
            return ctx.enter_context(nc.sbuf_tensor(name, shape, dt))

        def ps(name, shape):
            return ctx.enter_context(nc.psum_tensor(name, shape, F32))

        def sem(name):
            return ctx.enter_context(nc.semaphore(name))

        def sems(name, n):
            return [sem(f"{name}{i}") for i in range(n)]

        ident = sb("ident", [P, P])
        att_sum = sb("att_sum", [P, P])
        att_pos = sb("att_pos", [P, P])
        att_col = sb("att_col", [P, 1])
        wl_rows = sb("wl_rows", [P, P])
        wr_rows = sb("wr_rows", [P, P])
        wlT = sb("wlT", [P, P])
        wrT = sb("wrT", [P, P])
        bias_all = sb("bias_all", [P, P])
        eps_col = sb("eps_col", [P, 1])
        we1 = sb("we1", [EC, P])
        we2 = sb("we2", [P, P])
        wt_col = sb("wt_col", [P, 1])
        wn1a = sb("wn1a", [P, P])
        wn1b = sb("wn1b", [P, P])
        wn2 = sb("wn2", [P, P])
        cols = sb("cols", [P, 5])
        half = sb("half", [P, 3])
        work = sb("work", [P, 8, ROWS * P])
        xc = work[:, 0:4]
        yc = work[:, 4:8]
        xn = work[:, 0].rearrange("p (b s e) -> p b s e", b=2, s=2)
        hT = work[:, 1].rearrange("p (b s e) -> p b s e", b=2, s=2)
        xsum, xpos, mc, delta = (work[:, 2, k * GE:(k + 1) * GE] for k in range(4))
        dd = work[:, 3, 0:2 * GE].rearrange("p (k e) -> p k e", k=2)
        pp = work[:, 3, 2 * GE:4 * GE].rearrange("p (k e) -> p k e", k=2)
        accT = work[:, 4, 0:2 * GE].rearrange("p (k e) -> p k e", k=2)
        denT = work[:, 4, 2 * GE:4 * GE].rearrange("p (k e) -> p k e", k=2)
        px, attn = work[:, 5, 0:GE], work[:, 5, GE:2 * GE]
        gate = work[:, 6].rearrange("p (g e) -> p g e", g=4)
        ew = work[:, 7]
        y_rows = [work[:, k, j * GE:(j + 1) * GE] for k in (4, 5) for j in (2, 3)]
        eT = work[0:EC, 1, 3 * GE:4 * GE]
        rows_i = sb("rows_i", [P, 5, 2, P], I32)
        rows_f = sb("rows_f", [P, 3, 2, P])
        keep_r = sb("keep_r", [P, 2, P])
        flag_r = sb("flag_r", [P, 2, 2, P], BF16)
        table = sb("table", [P, NG, 3, TILES], I32)
        gidx = sb("gidx", [P, 4, 2, TILES], I32)
        sidx = sb("sidx", [P, 4, TILES], I32)
        x1 = sb("x1", [P, NG, GE])
        xg = sb("xg", [P, 4, 2, GE])
        stat = sb("stat", [P, 2, 16, 6])
        mean2 = sb("mean2", [P, 2, 16])
        dmean = sb("dmean", [P, 2, 16])
        m2 = sb("m2", [P, 2, 16])
        var = sb("var", [P, 2, 16])
        lnv = sb("lnv", [P, 16])
        rstd = sb("rstd", [P, 2, 16])
        nmr = sb("nmr", [P, 2, 16])
        cap = sb("cap", [P, 4, GE], BF16)
        carry = sb("carry", [P, 1])
        rden = sb("rden", [P, TILES * H])
        ea = rows_i[:, 0:4].rearrange("p b s (t d) -> p b (s t) d", d=EC).bitcast(F32)

        psT = ps("psT", [P, 2, GE])
        psL = ps("psL", [P, 2, GE])
        psS = ps("psS", [P, GE])
        psA = ps("psA", [P, GE])
        psO = ps("psO", [P, GE])
        psD = ps("psD", [P, GE])

        block = ctx.enter_context(nc.Block())

        s_pool_go = sem("pool_goes_on")
        s_sp_go = sem("sp_goes_on")
        s_pe_go = sem("pe_goes_on")
        s_load = sem("weights_in")
        s_pad = sem("pads_set")
        s_rows = sem("edge_rows_in")
        s_const = sem("constants_set")
        s_ident = sem("ident_set")
        s_mix = sem("att_mix_set")
        s_zero = sem("carry_set")
        s_fl = sem("flags_made")
        s_flag_out = sem("flags_out")
        s_setT = sem("setup_transposed")
        s_table = sem("table_ready")
        idx_in = sems("idx_in", 4)
        cap_in = sems("cap_in", 4)
        copied = sems("table_copied", 2)
        got = sems("rows_gathered", 4)
        parked = sems("x_parked", 4)
        s_stat = sem("stats_done")
        s_var = sem("var_done")
        s_rstd = sem("rstd_done")
        s_ln = sem("ln_done")
        s_nmr = sem("nmr_done")
        s_xn = sem("norm_done")
        s_T = sem("h_turned")
        s_hT = sem("h_copied")
        s_S = sem("products_done")
        s_xs = sem("sum_copied")
        s_A = sem("scores_done")
        s_mc = sem("max_steps")
        s_dl = sem("delta_done")
        s_dd = sem("exponents_done")
        s_pp = sem("exp_done")
        s_px = sem("weighted_done")
        s_acc = sem("sums_done")
        s_O = sem("sums_turned")
        s_rd = sem("den_steps")
        s_att = sem("attention_rows")
        s_x1 = sem("x1_done")
        idx2_in = sems("idx2_in", 4)
        chunk_in = sems("chunk_in", 4)
        s_xb = sem("chunk_biased")
        s_stat2 = sem("chunk_stats")
        s_var2 = sem("chunk_var")
        s_ln2 = sem("chunk_ln")
        s_rstd2 = sem("chunk_rstd")
        s_nmr2 = sem("chunk_nmr")
        s_n2 = sem("chunk_norm")
        s_y2 = sem("chunk_done")
        chunk_out = sems("chunk_out", 4)
        s_stage = sem("x1_staged")
        x1_out = sems("x1_scattered", 4)
        idx3_in = sems("idx3_in", 4)
        sidx3_in = sems("scatter_idx3_in", 4)
        in3 = sems("edges_in", 4)
        ew_in = sem("weights_of_edges_in")
        got3 = sems("x1_gathered", 4)
        s_xb3 = sem("rows_biased")
        s_stat3 = sem("stats3")
        s_var3 = sem("var3")
        s_ln3 = sem("ln3")
        s_rstd3 = sem("rstd3")
        s_nmr3 = sem("nmr3")
        s_xn3 = sem("norm3")
        s_nd = sem("destinations_normed")
        s_y0 = sem("y0_done")
        s_T3 = sem("turned3")
        s_hT3 = sem("h2_copied")
        s_Te = sem("attributes_turned")
        s_eT = sem("attributes_copied")
        s_m1 = sem("mm_edge1")
        s_h1 = sem("h1_done")
        s_m2 = sem("mm_edge2")
        s_ef = sem("ef_done")
        s_tw = sem("tanh_done")
        s_gt = sem("gated_done")
        s_m3 = sem("mm_node1")
        s_r = sem("r_done")
        s_m4 = sem("mm_node2")
        s_msg = sem("msg_done")
        s_sum = sem("msg_sums")
        s_O3 = sem("msg_turned")
        s_y3 = sem("y_done")
        y_out = sems("y_scattered", 4)

        N_WEIGHTS = 11 + 5 - 1
        keep_rows = keep_d.rearrange("(t e) -> t e", e=P)
        cap_rows = cap_d.rearrange("(t e) -> t e", e=P)

        def uses(r, c):
            return r + c // 4

        def pair_uses(r, c):
            return 2 * r + c // 2

        def load_rows(dma, kinds):
            for k, (a, shift) in kinds:
                lo = 1 if shift == -1 else 0
                hi = 1 if shift == 1 else 0
                if lo:
                    dma(rows_i[0:1, k, 0, 1:P], a[0:P - 1].rearrange("(a b) -> a b", a=1)).then_inc(s_rows, 16)
                    dma(rows_i[1:P, k, 0, :], a[P - 1:TA * P - 1].rearrange("(a b) -> a b", b=P)).then_inc(s_rows, 16)
                else:
                    dma(rows_i[:, k, 0, :], a[shift:TA * P + shift].rearrange("(a b) -> a b", b=P)).then_inc(s_rows, 16)
                at = TA * P + shift
                dma(rows_i[0:FULL_B, k, 1, :], a[at:at + FULL_B * P].rearrange("(a b) -> a b", b=P)).then_inc(s_rows, 16)
                at += FULL_B * P
                dma(rows_i[FULL_B:FULL_B + 1, k, 1, 0:REST - hi],
                    a[at:at + REST - hi].rearrange("(a b) -> a b", a=1)).then_inc(s_rows, 16)

        kinds = list(enumerate(((dst, 0), (dst, -1), (dst, 1), (src, 0), (dst, 0))))

        @block.sync
        def _(sp):
            dma = sp.dma_start
            sp.wait_ge(s_pad, 5)
            load_rows(dma, kinds[:2])
            sp.wait_ge(s_fl, 4)
            for k, d in enumerate((keep_rows, cap_rows)):
                dma(d[0:TA, :], flag_r[:, k, 0, :]).then_inc(s_flag_out, 16)
                dma(d[TA:NT, :], flag_r[0:TB, k, 1, :]).then_inc(s_flag_out, 16)
            sp.wait_ge(s_table, 1)

            def copy_chunk(r, c):
                at = r * (4 * CH) + c * CH if not (known(r) and 4 * r + c == NC - 1) else N - CH
                if later(r, c, 2):
                    sp.wait_ge(copied[c % 2], 16 * pair_uses(r, c))
                if known(r) and 4 * r + c == NC - 1:
                    sp.wait_ge(copied[(c - 1) % 2], 16 * (pair_uses(r, c - 1) + 1))
                dma(x_tab[bass.ds(at, CH), :].rearrange("(p k) d -> p (k d)", p=P),
                    x[bass.ds(at, CH), :].rearrange("(p k) d -> p (k d)", p=P)).then_inc(copied[c % 2], 16)

            def phase1(r, c):
                c += 2
                if known(r) and 4 * r + c == NG:
                    park(r, c - 1)
                if live(r, c, NG):
                    b = c % 4
                    if later(r, c, 4):
                        sp.wait_ge(got[b], 16 * 2 * TILES * uses(r, c))
                    sp.sem_inc(s_sp_go, 1)
                    dma(gidx[:, b], table[:, bass.ds(r * 4 + c, 1), 0:2].rearrange("p a k t -> p (a k) t")).then_inc(idx_in[b], 16)
                    if later(r, c, 4):
                        sp.wait_ge(s_dd, r * 4 + c - 3)
                    else:
                        sp.wait_ge(s_flag_out, 64)
                    dma(cap[:, b], cap_d[bass.ds(r * 4 * GE + c * GE, GE)].rearrange("(a e) -> a e", a=1)
                        .to_broadcast([P, GE])).then_inc(cap_in[b], 16)
                    copy_chunk(r, c)
                    park(r, c - 1)
            def park(r, c):
                if live(r, c, NG):
                    b = c % 4
                    sp.wait_ge(got[b], 16 * 2 * TILES * (uses(r, c) + 1))
                    dma(x1[:, bass.ds(r * 4 + c, 1)].rearrange("p a e -> p (a e)"), xg[:, b, 1, :]).then_inc(parked[b], 16)

            run_steps(sp, phase1, NG)

            def chunk_rows(tensor, r, c):
                at = N - CH if known(r) and 4 * r + c == NC - 1 else r * (4 * CH) + c * CH
                return tensor[bass.ds(at, CH), :].rearrange("(p k) d -> p (k d)", p=P)

            def load_scatter_rows(r, c, arrived):
                dma(sidx[:, c % 4], table[:, bass.ds(r * 4 + c, 1), 2].rearrange("p a t -> p (a t)")).then_inc(arrived[c % 4], 16)

            def load_gather_rows(r, c):
                if live(r, c, NG):
                    if later(r, c, 4):
                        sp.wait_ge(got3[c % 4], 16 * TILES * uses(r, c))
                    else:
                        sp.wait_ge(got[c % 4], 16 * 2 * TILES * ((NG - 1 - c % 4) // 4 + 1))
                    sp.sem_inc(s_sp_go, 1)
                    dma(gidx[:, c % 4], table[:, bass.ds(r * 4 + c, 1), 0:2].rearrange("p a k t -> p (a k) t")).then_inc(idx3_in[c % 4], 16)

            def load_edges(r, c):
                if live(r, c, NG):
                    b = c % 4
                    if later(r, c, 4):
                        sp.wait_ge(s_sum, r * 4 + c - 3)
                        sp.sem_inc(s_sp_go, 1)
                    dma(cap[:, b], keep_d[bass.ds(r * 4 * GE + c * GE, GE)].rearrange("(a e) -> a e", a=1)
                        .to_broadcast([P, GE])).then_inc(in3[b], 16)
                    if known(r) and 4 * r + c == NG - 1:
                        at, full = (NG - 1) * GE, (E - (NG - 1) * GE) // P
                        dma(ea[:, b, 0:full], edge_attr[at:at + full * P, :].rearrange("(t p) d -> p t d", p=P)).then_inc(in3[b], 16)
                        dma(ea[0:REST, b, full], edge_attr[at + full * P:E, :]).then_inc(in3[b], 16)
                    else:
                        dma(ea[:, b], edge_attr[bass.ds(r * 4 * GE + c * GE, GE), :].rearrange("(t p) d -> p t d", p=P)).then_inc(in3[b], 16)

            load_scatter_rows(0, 0, idx2_in)
            load_scatter_rows(0, 1, idx2_in)

            def phase2(r, c):
                g = c + 2
                if live(r, g, NC):
                    b = g % 4
                    if later(r, g, 4):
                        sp.wait_ge(s_y2, r * 4 + g - 3)
                    else:
                        sp.wait_ge((s_T, s_S, s_x1, s_x1)[g], NG)
                    dma(xc[:, b], chunk_rows(x, r, g)).then_inc(chunk_in[b], 16)
                g = c + 4
                if live(r, g, NG) and not (known(r) and 4 * r + g < 2):
                    if later(r, g, 4):
                        sp.wait_ge(x1_out[g % 4], 16 * TILES * uses(r, g))
                        sp.sem_inc(s_sp_go, 1)
                    load_scatter_rows(r, g, idx2_in)
                g = c - 2
                if live(r, g, NC):
                    sp.wait_ge(s_y2, r * 4 + g + 1)
                    if known(r) and 4 * r + g == NC - 1:
                        sp.wait_ge(chunk_out[(g - 1) % 4], 16 * (uses(r, g - 1) + 1))
                    dma(chunk_rows(out, r, g), yc[:, g % 4]).then_inc(chunk_out[g % 4], 16)
                if known(r) and 4 * r + c == NC - 3:
                    for k in range(4):
                        load_gather_rows(0, k)
                    for k in range(3):
                        load_edges(0, k)

            run_steps(sp, phase2, NG)

            def phase3(r, c):
                if not (known(r) and 4 * r + c < 0):
                    load_gather_rows(r, c + 4)
                    load_edges(r, c + 3)
                    if live(r, c, NG):
                        if later(r, c, 4):
                            sp.wait_ge(y_out[c % 4], 16 * TILES * uses(r, c))
                        else:
                            sp.wait_ge(x1_out[c % 4], 16 * TILES * ((NG - 1 - c % 4) // 4 + 1))
                        sp.sem_inc(s_sp_go, 1)
                        load_scatter_rows(r, c, sidx3_in)
                        if c % 4 == 0:
                            load_weights(r, c + 4)

            def load_weights(r, c):
                if live(r, c, NG):
                    if later(r, c, 1):
                        sp.wait_ge(s_tw, uses(r, c))
                    n = min(4 * GE, E - (4 * r + c) * GE) if known(r) else 4 * GE
                    dma(ew[:, 0:n], edge_weight[bass.ds(r * 4 * GE + c * GE, n)].rearrange("(a e) -> a e", a=1)
                        .to_broadcast([P, n])).then_inc(ew_in, 16)

            sp.wait_ge(chunk_out[3], 16 * ((NC - 1 - 3) // 4 + 1))
            load_weights(0, 0)
            run_steps(sp, phase3, NG)
            for b in range(2):
                sp.wait_ge(copied[b], 16 * ((NC - 1 - b) // 2 + 1))
            for b in range(4):
                sp.wait_ge(chunk_out[b], 16 * ((NC - 1 - b) // 4 + 1))
                sp.wait_ge(x1_out[b], 16 * TILES * ((NG - 1 - b) // 4 + 1))
                sp.wait_ge(y_out[b], 16 * TILES * ((NG - 1 - b) // 4 + 1))

        def arrived3(r, c):
            per = 16 * 2
            return per * (uses(r, c) + 1) + (16 if known(r) and 4 * r + c == NG - 1 else 0)

        @block.gpsimd
        def _(pool):
            for k, v in enumerate((0, -1, -1, 0, NOWHERE)):
                pool.memset(rows_i[:, k], v).then_inc(s_pad, 1)
            pool.memset(ident[:, :], 0.0).then_inc(s_const, 1)
            pool.memset(att_pos[:, :], 1.0).then_inc(s_const, 1)
            pool.wait_ge(s_const, 2)
            pool.affine_select(out=ident[:, :], in_=ident[:, :], compare_op=ALU.not_equal, fill=1.0,
                               base=0, pattern=[[-1, P]], channel_multiplier=1).then_inc(s_ident, 1)
            heads = att_pos[:, :].rearrange("p (h c) -> p h c", c=C)
            pool.affine_select(out=heads, in_=heads, compare_op=ALU.is_ge, fill=0.0,
                               base=0, pattern=[[-C, H], [0, C]], channel_multiplier=1).then_inc(s_mix, 1)
            pool.wait_ge(s_mix, 1)
            pool.affine_select(out=heads, in_=heads, compare_op=ALU.is_ge, fill=0.0,
                               base=C - 1, pattern=[[C, H], [0, C]], channel_multiplier=-1).then_inc(s_mix, 1)

            def phase1(r, c):
                c += 2
                if live(r, c, NG):
                    b = c % 4
                    pool.wait_ge(idx_in[b], 16 * (uses(r, c) + 1))
                    if later(r, c, 4):
                        pool.wait_ge(s_xn, r * 4 + c - 3)
                        pool.wait_ge(parked[b], 16 * uses(r, c))
                    pool.sem_inc(s_pool_go, 1)
                    for j in range(TILES):
                        for side in range(2):
                            pool.indirect_dma_start(
                                out=xg[:, b, side, j * P:(j + 1) * P], out_offset=None, in_=x,
                                in_offset=bass.IndirectOffsetOnAxis(ap=gidx[:, b, side, j:j + 1], axis=0)
                            ).then_inc(got[b], 16)

            pool.wait_ge(s_table, 1)
            run_steps(pool, phase1, NG)

            for b in range(2):
                pool.wait_ge(copied[b], 16 * ((NC - 1 - b) // 2 + 1))

            def phase2(r, c):
                c += 2
                if live(r, c, NG):
                    b = c % 4
                    pool.wait_ge(idx2_in[b], 16 * (uses(r, c) + 1))
                    pool.wait_ge(s_stage, r * 4 + c + 1)
                    pool.sem_inc(s_pool_go, 1)
                    for j in range(TILES):
                        pool.indirect_dma_start(
                            out=x_tab, out_offset=bass.IndirectOffsetOnAxis(ap=sidx[:, b, j:j + 1], axis=0),
                            in_=xg[:, b, 1, j * P:(j + 1) * P], in_offset=None,
                            bounds_check=N - 1, oob_is_err=False).then_inc(x1_out[b], 16)

            run_steps(pool, phase2, NG)

            for b in range(4):
                pool.wait_ge(x1_out[b], 16 * TILES * ((NG - 1 - b) // 4 + 1))

            def gather_x1(r, g):
                if live(r, g, NG):
                    b = g % 4
                    pool.wait_ge(idx3_in[b], 16 * (uses(r, g) + 1))
                    if later(r, g, 4):
                        pool.wait_ge(s_xn3, r * 4 + g - 3)
                    pool.sem_inc(s_pool_go, 1)
                    for j in range(TILES):
                        pool.indirect_dma_start(
                            out=xg[:, b, 0, j * P:(j + 1) * P], out_offset=None, in_=x_tab,
                            in_offset=bass.IndirectOffsetOnAxis(ap=gidx[:, b, 0, j:j + 1], axis=0)
                        ).then_inc(got3[b], 16)

            def phase3(r, c):
                gather_x1(r, c + 3)
                g = c - 2
                if live(r, g, NG):
                    b = g % 4
                    if known(r) and 4 * r + g == 0:
                        for k in range(4):
                            pool.wait_ge(chunk_out[k], 16 * ((NC - 1 - k) // 4 + 1))
                    pool.wait_ge(sidx3_in[b], 16 * (uses(r, g) + 1))
                    pool.wait_ge(s_y3, r * 4 + g + 1)
                    pool.sem_inc(s_pool_go, 1)
                    for j in range(TILES):
                        pool.indirect_dma_start(
                            out=out, out_offset=bass.IndirectOffsetOnAxis(ap=sidx[:, b, j:j + 1], axis=0),
                            in_=y_rows[b][:, j * P:(j + 1) * P], in_offset=None,
                            bounds_check=N - 1, oob_is_err=False).then_inc(y_out[b], 16)

            gather_x1(0, 0)
            run_steps(pool, phase3, NG)

        def stats_rows(dve, rows, n, b, s_stats):
            for j in range(n):
                last = dve.bn_stats(stat[:, b, j, :], rows(j))
            last.then_inc(s_stats, 1)

        def stats_means(dve, n, b, s_stats, g):
            dve.wait_ge(s_stats, 3 * g + 1)
            dve.tensor_tensor(dmean[:, b, 0:n], stat[:, b, 0:n, 1], stat[:, b, 0:n, 4], ALU.subtract)
            dve.tensor_tensor(m2[:, b, 0:n], stat[:, b, 0:n, 2], stat[:, b, 0:n, 5], ALU.add)
            dve.tensor_tensor(mean2[:, b, 0:n], stat[:, b, 0:n, 1], stat[:, b, 0:n, 4], ALU.add).then_inc(s_stats, 1)

        def stats_square(dve, n, b, s_stats, g):
            dve.wait_ge(s_stats, 3 * g + 2)
            dve.tensor_tensor(dmean[:, b, 0:n], dmean[:, b, 0:n], dmean[:, b, 0:n], ALU.mult).then_inc(s_stats, 1)

        def stats_var(dve, n, b, s_stats, s_variance, g):
            dve.wait_ge(s_stats, 3 * g + 3)
            dve.scalar_tensor_tensor(out=var[:, b, 0:n], in0=dmean[:, b, 0:n], scalar=P / 4.0, in1=m2[:, b, 0:n],
                                     op0=ALU.mult, op1=ALU.add).then_inc(s_variance, 1)

        def negative_mean(dve, n, b):
            return dve.scalar_tensor_tensor(out=nmr[:, b, 0:n], in0=mean2[:, b, 0:n], scalar=-0.5,
                                            in1=rstd[:, b, 0:n], op0=ALU.mult, op1=ALU.mult)

        @block.vector
        def _(dve):
            dve.memset(eps_col[:, :], EPS)
            dve.memset(carry[:, :], 0.0).then_inc(s_zero, 1)
            dve.wait_ge(s_rows, 16 * 16)
            dve.tensor_tensor(keep_r[:, :, :], rows_i[:, 0], rows_i[:, 1], ALU.is_equal).then_inc(s_fl, 1)
            dve.tensor_tensor(rows_f[:, 2], rows_i[:, 0], rows_i[:, 2], ALU.is_equal).then_inc(s_fl, 1)
            dve.wait_ge(s_fl, 2)
            dve.tensor_copy(flag_r[:, 0], keep_r[:, :, :]).then_inc(s_fl, 1)
            dve.tensor_scalar(flag_r[:, 1], keep_r[:, :, :], 2 * BIG, -BIG, ALU.mult, ALU.add).then_inc(s_fl, 1)
            dve.tensor_copy(rows_f[:, 0], rows_i[:, 3])
            dve.tensor_copy(rows_f[:, 1], rows_i[:, 0])
            dve.scalar_tensor_tensor(out=rows_f[:, 2], in0=rows_f[:, 2], scalar=float(NOWHERE), in1=rows_i[:, 4],
                                     op0=ALU.mult, op1=ALU.add).then_inc(s_fl, 1)
            dve.wait_ge(s_setT, 1)
            turned = psT[:, :, :].rearrange("p a (k t) -> p (a k) t", t=P)
            for k in range(3):
                dve.tensor_copy(table[:, 0:TA // TILES, k, :],
                                turned[:, k, :].rearrange("p (g t) -> p g t", t=TILES))
            dve.wait_ge(s_setT, 2)
            turned = psL[:, :, :].rearrange("p a (k t) -> p (a k) t", t=P)
            for k in range(3):
                last = dve.tensor_copy(table[:, TA // TILES:NG, k, :],
                                       turned[:, k, 0:TB].rearrange("p (g t) -> p g t", t=TILES))
            last.then_inc(s_table, 1)
            dve.wait_ge(s_setT, 3)
            dve.tensor_copy(wlT[:, :], psS[:, 0:P])
            dve.tensor_copy(wrT[:, :], psS[:, P:2 * P])
            dve.wait_ge(s_load, 16 * N_WEIGHTS)
            dve.wait_ge(s_mix, 2)
            dve.wait_ge(s_zero, 1)
            dve.tensor_scalar(att_sum[:, :], att_pos[:, :], att_col[:, 0:1], NEG_SLOPE, ALU.mult, ALU.mult).then_inc(s_zero, 1)
            dve.wait_ge(s_zero, 2)
            dve.tensor_scalar(att_pos[:, :], att_pos[:, :], att_col[:, 0:1], 1 - NEG_SLOPE, ALU.mult, ALU.mult)
            dve.tensor_scalar(half[:, 2:3], wt_col[:, :], 0.5, None, ALU.mult)
            dve.tensor_scalar(half[:, 0:2], cols[:, 1:3], 0.5, None, ALU.mult).then_inc(s_table, 1)

            def phase1(r, c):
                g, b, h = r * 4 + c, c % 4, c % 2
                now, norm, before = live(r, c, NG), live(r, c + 2, NG), live(r, c - 1, NG)
                n, bn, bp = 2 * TILES, (c + 2) % 4, (c - 1) % 4
                if norm:
                    dve.wait_ge(got[bn], 16 * n * (uses(r, c + 2) + 1))
                    if later(r, c + 2, 2):
                        dve.wait_ge(s_xn, g + 1)
                    stats_rows(dve, lambda j: xg[:, bn, j // TILES, (j % TILES) * P:(j % TILES + 1) * P], n, h, s_stat)
                if now:
                    dve.wait_ge(cap_in[b], 16 * (uses(r, c) + 1))
                    dve.tensor_tensor(mc[:, 0:1], carry[:, :], cap[:, b, 0:1], ALU.min).then_inc(s_mc, 1)
                if norm:
                    stats_means(dve, n, h, s_stat, g + 2)
                if now:
                    dve.wait_ge(s_A, g + 1)
                    dve.wait_ge(s_mc, 3 * g + 1)
                    dve.tensor_tensor_scan(mc[:, 1:GE], psA[:, 0:GE - 1], cap[:, b, 1:GE], mc[:, 0:1],
                                           ALU.max, ALU.min).then_inc(s_mc, 1)
                if norm:
                    stats_square(dve, n, h, s_stat, g + 2)
                if now:
                    dve.wait_ge(s_mc, 3 * g + 2)
                    dve.tensor_tensor(delta[:, :], psA[:, :], mc[:, :], ALU.subtract).then_inc(s_dl, 1)
                if norm:
                    stats_var(dve, n, h, s_stat, s_var, g + 2)
                if now:
                    dve.tensor_tensor(carry[:, :], psA[:, GE - 1:GE], mc[:, GE - 1:GE], ALU.max).then_inc(s_mc, 1)
                    dve.wait_ge(s_dl, g + 1)
                    dve.tensor_scalar(dd[:, 0, :], delta[:, :], 0.0, -1.0, ALU.max, ALU.mult)
                    dve.tensor_scalar(dd[:, 1, :], delta[:, :], 0.0, None, ALU.min).then_inc(s_dd, 1)
                if norm:
                    dve.wait_ge(s_rstd, g + 3)
                    negative_mean(dve, n, h).then_inc(s_nmr, 1)
                if before:
                    dve.wait_ge(s_O, g)
                    dve.tensor_scalar(rden[:, :], psD[:, 0:GE:C], 1e-16, None, ALU.add).then_inc(s_rd, 1)
                if before:
                    dve.wait_ge(s_rd, 2 * g - 1)
                    dve.reciprocal(rden[:, :], rden[:, :]).then_inc(s_rd, 1)
                    dve.wait_ge(s_rd, 2 * g)
                    dve.tensor_tensor(attn[:, :].rearrange("p (k c) -> p k c", c=C),
                                      psO[:, :].rearrange("p (k c) -> p k c", c=C),
                                      rden[:, :].unsqueeze(2).to_broadcast([P, TILES * H, C]), ALU.mult).then_inc(s_att, 1)
                first = known(r) and r * 4 + c == 0
                if now:
                    dve.wait_ge(s_pp, g + 1)
                    dve.tensor_tensor(px[:, :], pp[:, 1, :], psL[:, h, :], ALU.mult).then_inc(s_px, 1)
                if before:
                    dve.wait_ge(parked[bp], 16 * (uses(r, c - 1) + 1))
                    dve.wait_ge(s_att, g)
                    row = x1[:, bass.ds(g - 1, 1)].rearrange("p a e -> p (a e)")
                    dve.tensor_tensor(row, attn[:, :], row, ALU.add).then_inc(s_x1, 1)
                if now:
                    if later(r, c, 2):
                        dve.wait_ge(s_O, g - 1)
                    if later(r, c, 1):
                        dve.wait_ge(s_acc, 2 * g)
                    dve.wait_ge(s_px, g + 1)
                    dve.tensor_tensor_scan(accT[:, h, :], pp[:, 0, :], px[:, :],
                                           0.0 if first else accT[:, 1 - h, GE - 1:GE], ALU.mult, ALU.add).then_inc(s_acc, 1)
                    dve.tensor_tensor_scan(denT[:, h, :], pp[:, 0, :], pp[:, 1, :],
                                           0.0 if first else denT[:, 1 - h, GE - 1:GE], ALU.mult, ALU.add).then_inc(s_acc, 1)

            run_steps(dve, phase1, NG)

            def phase2(r, c):
                g, h = r * 4 + c, c % 2
                b = c % 4
                rows = xc[:, b].rearrange("p (k d) -> p k d", d=D)
                now, after, before = live(r, c, NC), live(r, c + 1, NC), live(r, c - 2, NC)

                def add_up(part):
                    o, cut = (c - 2) % 4, slice(part * ROWS * P // 2, (part + 1) * ROWS * P // 2)
                    return dve.tensor_tensor(yc[:, o, cut], yc[:, o, cut], xc[:, o, cut], ALU.add)

                if now:
                    dve.wait_ge(s_xb, g + 1)
                    if later(r, c, 2):
                        dve.wait_ge(s_n2, g - 1)
                    stats_rows(dve, lambda j: rows[:, j, :], ROWS, h, s_stat2)
                if before:
                    dve.wait_ge(s_n2, g - 1)
                    add_up(0)
                if now:
                    stats_means(dve, ROWS, h, s_stat2, g)
                if before:
                    add_up(1).then_inc(s_y2, 1)
                if now:
                    stats_square(dve, ROWS, h, s_stat2, g)
                    stats_var(dve, ROWS, h, s_stat2, s_var2, g)
                if after:
                    bn = (c + 1) % 4
                    dve.wait_ge(chunk_in[bn], 16 * (uses(r, c + 1) + 1))
                    chunk = xc[:, bn].rearrange("p (k d) -> p k d", d=D)
                    dve.tensor_tensor(chunk, chunk, bias_all[:, :].unsqueeze(1).to_broadcast([P, ROWS, D]), ALU.add).then_inc(s_xb, 1)
                if now:
                    dve.wait_ge(s_rstd2, g + 1)
                    negative_mean(dve, ROWS, h).then_inc(s_nmr2, 1)

            run_steps(dve, phase2, NC)

            def phase3(r, c):
                g = r * 4 + c
                now, norm, after, before = live(r, c, NG), live(r, c + 2, NG), live(r, c + 1, NG), live(r, c - 1, NG)
                h, b, bn, ba, bp = c % 2, c % 4, (c + 2) % 4, (c + 1) % 4, (c - 1) % 4
                n = 2 * TILES
                bias_rows = bias_all[:, :].unsqueeze(1).to_broadcast([P, TILES, D])
                if norm:
                    dve.wait_ge(got3[bn], 16 * TILES * (uses(r, c + 2) + 1))
                    src_rows = xg[:, bn, 0, :].rearrange("p (k d) -> p k d", d=D)
                    dve.tensor_tensor(src_rows, src_rows, bias_rows, ALU.add).then_inc(s_xb3, 1)
                if after:
                    dve.wait_ge(s_rstd3, g + 2)
                    if later(r, c + 1, 2):
                        dve.wait_ge(s_xn3, g)
                    negative_mean(dve, n, 1 - h).then_inc(s_nmr3, 1)
                if norm:
                    if later(r, c + 2, 4):
                        dve.wait_ge(s_y3, g - 1)
                    dst_rows = xg[:, bn, 1, :].rearrange("p (k d) -> p k d", d=D)
                    dve.tensor_tensor(dst_rows, x1[:, bass.ds(g + 2, 1)].rearrange("p a (k d) -> p (a k) d", d=D), bias_rows, ALU.add).then_inc(s_xb3, 1)
                if after:
                    dve.wait_ge(s_nmr3, g + 2)
                    for k in range(TILES):
                        j, part = TILES + k, slice(k * P, (k + 1) * P)
                        last = dve.tensor_scalar(xn[:, 0, 1, part], xg[:, ba, 1, part], rstd[:, 1 - h, j:j + 1], nmr[:, 1 - h, j:j + 1],
                                                 ALU.mult, ALU.add)
                    last.then_inc(s_nd, 1)
                if before:
                    dve.wait_ge(s_y0, g)
                    dve.wait_ge(s_O3, g)
                    if later(r, c - 1, 4):
                        dve.wait_ge(y_out[bp], 16 * TILES * uses(r, c - 1))
                    dve.tensor_tensor(y_rows[bp], psO[:, :], xg[:, bp, 1, :], ALU.add).then_inc(s_y3, 1)
                if after:
                    dve.wait_ge(s_nd, g + 2)
                    dve.scalar_tensor_tensor(out=xg[:, ba, 1, :], in0=xn[:, 0, 1, :], scalar=0.0, in1=xg[:, ba, 1, :],
                                             op0=ALU.max, op1=ALU.add).then_inc(s_y0, 1)
                if norm:
                    dve.wait_ge(s_xb3, 2 * (g + 3))
                    stats_rows(dve, lambda j: xg[:, bn, j // TILES, (j % TILES) * P:(j % TILES + 1) * P], n, h, s_stat3)
                if after:
                    dve.wait_ge(s_ef, g + 2)
                    if (c + 1) % 4 == 0:
                        dve.wait_ge(s_tw, uses(r, c + 1) + 1)
                    if later(r, c + 1, 1):
                        dve.wait_ge(s_m3, g + 1)
                    dve.scalar_tensor_tensor(out=delta[:, :], in0=gate[:, ba, :], scalar=1.0, in1=pp[:, 1, :],
                                             op0=ALU.add, op1=ALU.mult).then_inc(s_gt, 1)
                if norm:
                    stats_means(dve, n, h, s_stat3, g + 2)
                if now:
                    dve.wait_ge(in3[b], arrived3(r, c))
                    dve.wait_ge(s_msg, g + 1)
                    if later(r, c, 1):
                        dve.wait_ge(s_sum, g)
                    if later(r, c, 2):
                        dve.wait_ge(s_O3, g - 1)
                    first = known(r) and r * 4 + c == 0
                    dve.tensor_tensor_scan(accT[:, h, :], cap[:, b, :], px[:, :],
                                           0.0 if first else accT[:, 1 - h, GE - 1:GE], ALU.mult, ALU.add).then_inc(s_sum, 1)
                if norm:
                    stats_square(dve, n, h, s_stat3, g + 2)
                    stats_var(dve, n, h, s_stat3, s_var3, g + 2)

            for b in range(2):
                dve.wait_ge(chunk_out[b], 16 * ((NC - 1 - b) // 4 + 1))
            run_steps(dve, phase3, NG)

        def make_scales(act, n, b, s_variance, s_log, s_scale, g):
            act.wait_ge(s_variance, g + 1)
            act.activation(lnv[:, 0:n], var[:, b, 0:n], ACT.Ln, scale=1.0 / P, bias=eps_col[:, 0:1]).then_inc(s_log, 1)
            act.wait_ge(s_log, g + 1)
            act.activation(rstd[:, b, 0:n], lnv[:, 0:n], ACT.Exp, scale=-0.5).then_inc(s_scale, 1)

        def normalise(act, rows_in, rows_out, blocks, b):
            for j in blocks:
                last = act.activation(rows_out(j), rows_in(j), ACT.Relu, scale=rstd[:, b, j:j + 1], bias=nmr[:, b, j:j + 1])
            return last

        @block.scalar
        def _(act):
            act.preload_act_table_set("natural_log_exp_and_others")
            act.wait_ge(s_pad, 5)
            load_rows(act.dma_start, kinds[2:])
            for tile, source in ((wl_rows, W_l), (wr_rows, W_r), (we1, We1), (we2, We2),
                                 (wt_col, Wt.rearrange("a d -> d a")), (wn1a, Wn1[0:P, :]), (wn1b, Wn1[P:2 * P, :]), (wn2, Wn2),
                                 (att_col, att.rearrange("h (c a) -> (h c) a", a=1)),
                                 (bias_all, bias0.rearrange("(a d) -> a d", a=1).to_broadcast([P, P]))):
                act.dma_start(tile[:, :], source).then_inc(s_load, 16)
            for k, source in enumerate((be1, be2, bt, bn1, bn2)):
                act.dma_start(cols[:, k:k + 1], source.rearrange("(d a) -> d a", a=1)).then_inc(s_load, 16)
            act.wait_ge(s_table, 2)

            def phase1(r, c):
                g, h = r * 4 + c, c % 2
                norm, b = live(r, c + 2, NG), (c + 2) % 4
                rows_in = lambda j: xg[:, b, j // TILES, (j % TILES) * P:(j % TILES + 1) * P]
                rows_out = lambda j: xn[:, h, j // TILES, (j % TILES) * P:(j % TILES + 1) * P]
                if live(r, c + 1, NG):
                    act.wait_ge(s_T, g + 2)
                    if later(r, c + 1, 2):
                        act.wait_ge(s_S, g)
                    act.copy(hT[:, 1 - h], psT[:, :, :]).then_inc(s_hT, 1)
                if norm:
                    make_scales(act, 2 * TILES, h, s_var, s_ln, s_rstd, g + 2)
                if live(r, c, NG):
                    act.wait_ge(s_dd, g + 1)
                    act.activation(pp[:, :, :], dd[:, :, :], ACT.Exp).then_inc(s_pp, 1)
                if norm:
                    act.wait_ge(s_nmr, g + 3)
                    if later(r, c + 2, 2):
                        act.wait_ge(s_T, g + 1)
                    normalise(act, rows_in, rows_out, range(TILES), h)
                if live(r, c + 1, NG):
                    act.wait_ge(s_S, g + 2)
                    if later(r, c + 1, 1):
                        act.wait_ge(s_A, g + 1)
                    act.copy(xsum[:, :], psS[:, :])
                    act.activation(xpos[:, :], psS[:, :], ACT.Relu).then_inc(s_xs, 1)
                if norm:
                    normalise(act, rows_in, rows_out, range(TILES, 2 * TILES), h).then_inc(s_xn, 1)

            run_steps(act, phase1, NG)

            act.wait_ge(s_x1, NG)

            def phase2(r, c):
                g, h = r * 4 + c, c % 2
                if live(r, c + 2, NG):
                    b = (c + 2) % 4
                    if later(r, c + 2, 4):
                        act.wait_ge(x1_out[b], 16 * TILES * uses(r, c + 2))
                    act.copy(xg[:, b, 1, :], x1[:, bass.ds(g + 2, 1)].rearrange("p a e -> p (a e)")).then_inc(s_stage, 1)
                if live(r, c, NC):
                    b = c % 4
                    make_scales(act, ROWS, h, s_var2, s_ln2, s_rstd2, g)
                    act.wait_ge(s_nmr2, g + 1)
                    if later(r, c, 4):
                        act.wait_ge(chunk_out[b], 16 * uses(r, c))
                    rows = xc[:, b].rearrange("p (k d) -> p k d", d=D)
                    normed = yc[:, b].rearrange("p (k d) -> p k d", d=D)
                    normalise(act, lambda j: rows[:, j, :], lambda j: normed[:, j, :], range(ROWS), h).then_inc(s_n2, 1)

            run_steps(act, phase2, NG)
            act.wait_ge(s_y2, NC)
            for b in (1, 2):
                act.wait_ge(chunk_out[b], 16 * ((NC - 1 - b) // 4 + 1))

            def phase3(r, c):
                g, h = r * 4 + c, c % 2
                now, after, b = live(r, c, NG), live(r, c + 1, NG), (c + 1) % 4
                rows_in = lambda j: xg[:, b, j // TILES, (j % TILES) * P:(j % TILES + 1) * P]
                rows_out = lambda j: xn[:, 1 - h, j // TILES, (j % TILES) * P:(j % TILES + 1) * P]
                if after:
                    act.wait_ge(s_Te, g + 2)
                    if later(r, c + 1, 1):
                        act.wait_ge(s_m1, g + 1)
                    act.copy(eT[:, :], psT[0:EC, 1, :]).then_inc(s_eT, 1)
                if now:
                    act.wait_ge(s_T3, g + 1)
                    if later(r, c, 1):
                        act.wait_ge(s_m3, g)
                    act.copy(hT[:, 0, 0, :], psT[:, 0, :]).then_inc(s_hT3, 1)
                if after:
                    make_scales(act, 2 * TILES, 1 - h, s_var3, s_ln3, s_rstd3, g + 1)
                    act.wait_ge(s_nmr3, g + 2)
                    if later(r, c + 1, 2):
                        act.wait_ge(s_T3, g)
                    normalise(act, rows_in, rows_out, range(TILES), 1 - h).then_inc(s_xn3, 1)
                if after and (c + 1) % 4 == 0:
                    n = min(4, NG - 4 * r - c - 1) if known(r) else 4
                    act.wait_ge(ew_in, 16 * (uses(r, c + 1) + 1))
                    if later(r, c + 1, 1):
                        act.wait_ge(s_gt, g + 1)
                    act.activation(gate[:, 0:n, :], ew[:, 0:n * GE], ACT.Tanh, scale=half[:, 2:3], bias=half[:, 1:2]).then_inc(s_tw, 1)
                    act.preload_act_table_set("natural_log_exp_and_others")
                if after:
                    act.wait_ge(s_m1, g + 2)
                    act.activation(dd[:, 0, :], psS[:, :], ACT.Relu, bias=cols[:, 0:1]).then_inc(s_h1, 1)
                if now:
                    act.wait_ge(s_m3, g + 1)
                    act.activation(dd[:, 1, :], psL[:, 1, :], ACT.Relu, bias=cols[:, 3:4]).then_inc(s_r, 1)
                if after:
                    act.wait_ge(s_m2, g + 2)
                    if later(r, c + 1, 1):
                        act.wait_ge(s_gt, g + 1)
                    act.activation(pp[:, 1, :], psA[:, :], ACT.Identity, scale=0.5, bias=half[:, 0:1]).then_inc(s_ef, 1)
                if now:
                    act.wait_ge(s_m4, g + 1)
                    if later(r, c, 1):
                        act.wait_ge(s_sum, g)
                    act.activation(px[:, :], psD[:, :], ACT.Identity, bias=cols[:, 4:5]).then_inc(s_msg, 1)

            run_steps(act, phase3, NG)

        @block.tensor
        def _(pe):
            pe.wait_ge(s_ident, 1)
            pe.wait_ge(s_fl, 5)
            for half_, n, to in ((0, TA, psT), (1, TB, psL)):
                for k in range(3):
                    last = pe.transpose(to[:, k // TILES, k * P:k * P + n], rows_f[0:n, k, half_, :], ident[0:n, 0:n])
                last.then_inc(s_setT, 1)
            pe.wait_ge(s_load, 16 * N_WEIGHTS)
            pe.transpose(psS[:, 0:P], wl_rows[:, :], ident[:, :])
            pe.transpose(psS[:, P:2 * P], wr_rows[:, :], ident[:, :]).then_inc(s_setT, 1)
            pe.wait_ge(s_table, 2)

            def phase1(r, c):
                g, h = r * 4 + c, c % 2
                if live(r, c + 1, NG):
                    pe.wait_ge(s_xn, g + 2)
                    if later(r, c + 1, 1):
                        pe.wait_ge(s_hT, g + 1)
                    for side in range(2):
                        for j in range(TILES):
                            last = pe.transpose(psT[:, side, j * P:(j + 1) * P], xn[:, 1 - h, side, j * P:(j + 1) * P], ident[:, :])
                    last.then_inc(s_T, 1)
                if live(r, c - 1, NG):
                    pe.wait_ge(s_acc, 2 * g)
                    if later(r, c - 1, 1):
                        pe.wait_ge(s_att, g - 1)
                    for j in range(TILES):
                        pe.transpose(psD[:, j * P:(j + 1) * P], denT[:, 1 - h, j * P:(j + 1) * P], ident[:, :])
                    for j in range(TILES):
                        last = pe.transpose(psO[:, j * P:(j + 1) * P], accT[:, 1 - h, j * P:(j + 1) * P], ident[:, :])
                    last.then_inc(s_O, 1)
                if live(r, c + 1, NG):
                    pe.wait_ge(s_hT, g + 2)
                    if later(r, c + 1, 2):
                        pe.wait_ge(s_px, g)
                    if later(r, c + 1, 1):
                        pe.wait_ge(s_xs, g + 1)
                    pe.matmul(psS[:, :], wlT[:, :], hT[:, 1 - h, 0, :], start=True, stop=False)
                    pe.matmul(psS[:, :], wrT[:, :], hT[:, 1 - h, 1, :], start=False, stop=True)
                    pe.matmul(psL[:, 1 - h, :], wlT[:, :], hT[:, 1 - h, 0, :], start=True, stop=True).then_inc(s_S, 1)
                    pe.wait_ge(s_xs, g + 2)
                    if later(r, c + 1, 1):
                        pe.wait_ge(s_dd, g + 1)
                    pe.matmul(psA[:, :], att_sum[:, :], xsum[:, :], start=True, stop=False)
                    pe.matmul(psA[:, :], att_pos[:, :], xpos[:, :], start=False, stop=True).then_inc(s_A, 1)

            run_steps(pe, phase1, NG)
            pe.wait_ge(s_x1, NG)

            def phase3(r, c):
                g, h = r * 4 + c, c % 2
                now, after, norm = live(r, c, NG), live(r, c + 1, NG), live(r, c + 2, NG)
                if live(r, c - 1, NG):
                    pe.wait_ge(s_sum, g)
                    if later(r, c - 1, 1):
                        pe.wait_ge(s_y3, g - 1)
                    for j in range(TILES):
                        last = pe.transpose(psO[:, j * P:(j + 1) * P], accT[:, 1 - h, j * P:(j + 1) * P], ident[:, :])
                    last.then_inc(s_O3, 1)
                if after:
                    pe.wait_ge(s_eT, g + 2)
                    if later(r, c + 1, 1):
                        pe.wait_ge(s_h1, g + 1)
                    pe.matmul(psS[:, :], we1[:, :], eT[:, :], start=True, stop=True).then_inc(s_m1, 1)
                if now:
                    pe.wait_ge(s_hT3, g + 1)
                    pe.wait_ge(s_gt, g + 1)
                    if later(r, c, 1):
                        pe.wait_ge(s_r, g)
                    pe.matmul(psL[:, 1, :], wn1a[:, :], hT[:, 0, 0, :], start=True, stop=False)
                    pe.matmul(psL[:, 1, :], wn1b[:, :], delta[:, :], start=False, stop=True).then_inc(s_m3, 1)
                if after:
                    pe.wait_ge(s_xn3, g + 2)
                    if later(r, c + 1, 1):
                        pe.wait_ge(s_hT3, g + 1)
                    for j in range(TILES):
                        last = pe.transpose(psT[:, 0, j * P:(j + 1) * P], xn[:, 1 - h, 0, j * P:(j + 1) * P], ident[:, :])
                    last.then_inc(s_T3, 1)
                    pe.wait_ge(s_h1, g + 2)
                    if later(r, c + 1, 1):
                        pe.wait_ge(s_ef, g + 1)
                    pe.matmul(psA[:, :], we2[:, :], dd[:, 0, :], start=True, stop=True).then_inc(s_m2, 1)
                if now:
                    pe.wait_ge(s_r, g + 1)
                    if later(r, c, 1):
                        pe.wait_ge(s_msg, g)
                    pe.matmul(psD[:, :], wn2[:, :], dd[:, 1, :], start=True, stop=True).then_inc(s_m4, 1)
                if norm:
                    b = (c + 2) % 4
                    pe.wait_ge(in3[b], arrived3(r, c + 2))
                    if later(r, c + 2, 1):
                        pe.wait_ge(s_eT, g + 2)
                    pe.sem_inc(s_pe_go, 1)
                    for j in range(TILES):
                        last = pe.transpose(psT[0:EC, 1, j * P:(j + 1) * P], ea[:, b, j, :], ident[:, :])
                    last.then_inc(s_Te, 1)

            run_steps(pe, phase3, NG)


_INS = ['x', 'src', 'dst', 'edge_attr_64', 'edge_weight', 'L0_gnn_W_l', 'L0_gnn_W_r', 'L0_gnn_att', 'L0_gnn_bias',
        'L1_gnn_We1', 'L1_gnn_be1', 'L1_gnn_We2', 'L1_gnn_be2', 'L1_gnn_Wt', 'L1_gnn_bt',
        'L1_gnn_Wn1', 'L1_gnn_bn1', 'L1_gnn_Wn2', 'L1_gnn_bn2']


def kernel(**inputs):
    import numpy as _np
    import concourse.bacc as _bacc
    from concourse.bass_utils import run_bass_kernel_spmd as _run

    nc = _bacc.Bacc("TRN2", target_bir_lowering=False, num_devices=1)
    arrays, args = {}, []
    for name in _INS:
        a = _np.ascontiguousarray(inputs[name])
        arrays[f"in_{name}"] = a
        args.append(nc.dram_tensor(f"in_{name}", a.shape, mybir.dt.from_np(a.dtype), kind="ExternalInput").ap())
    out = nc.dram_tensor("out_0", arrays["in_x"].shape, F32, kind="ExternalOutput").ap()
    gnn_program(nc, *args, out)
    r = _run(nc, [arrays], core_ids=[0])
    return r.results[0]["out_0"]
```

```python
from contextlib import ExitStack

import concourse.bass as bass
from concourse import mybir

F32 = mybir.dt.float32
BF16 = mybir.dt.bfloat16
I32 = mybir.dt.int32
ALU = mybir.AluOpType
ACT = mybir.ActivationFunctionType

P = 128
TILES = 4
GE = TILES * P
EPS = 1e-5
LEAST = -44.0
NEG_SLOPE = 0.2
BIG = float(2 ** 100)
NOWHERE = 2 ** 17
ROWS = 16
AHEAD, BEHIND = 2, 2


def known(r):
    return isinstance(r, int)


def live(r, c, count):
    return not known(r) or 0 <= 4 * r + c < count


def later(r, c, d):
    return not known(r) or 4 * r + c >= d


def loop_turns(count):
    return (count - AHEAD) // 4 - 1


def run_steps(eng, step, count):
    turns = loop_turns(count)
    for c in range(-AHEAD, 4):
        step(0, c)
    with eng.Fori(1, 1 + turns) as r:
        for c in range(4):
            step(r, c)
    for c in range(4 * (1 + turns), count + BEHIND):
        step(0, c)


def gnn_program(nc, x, src, dst, edge_attr, edge_weight, W_l, W_r, att, bias0,
                We1, be1, We2, be2, Wt, bt, Wn1, bn1, Wn2, bn2, out):
    N, D = x.shape
    E = src.shape[0]
    EC = edge_attr.shape[1]
    H, C = att.shape
    NT = -(-E // P)
    NG = -(-NT // TILES)
    assert D == P and H * C == P and NT == NG * TILES and 2 * P >= NT > P
    TA, TB = P, NT - P
    FULL_B, REST = E // P - P, E % P
    CH = P * ROWS
    NC = -(-N // CH)
    assert NC == NG and NG >= 12
    x_tab = nc.dram_tensor("x1_table", (N, D), F32).ap()
    src_o = nc.dram_tensor("src_ordered", (E,), I32).ap()
    dst_o = nc.dram_tensor("dst_ordered", (E,), I32).ap()
    weight_o = nc.dram_tensor("edge_weight_ordered", (E,), F32).ap()
    attr_o = nc.dram_tensor("edge_attr_ordered", (E, EC), F32).ap()
    keep_d = nc.dram_tensor("keep_flags", (NT * P,), BF16).ap()
    cap_d = nc.dram_tensor("max_caps", (NT * P,), BF16).ap()

    with ExitStack() as ctx:
        def sb(name, shape, dt=F32):
            return ctx.enter_context(nc.sbuf_tensor(name, shape, dt))

        def ps(name, shape):
            return ctx.enter_context(nc.psum_tensor(name, shape, F32))

        def sem(name):
            return ctx.enter_context(nc.semaphore(name))

        def sems(name, n):
            return [sem(f"{name}{i}") for i in range(n)]

        ident = sb("ident", [P, P])
        att_sum = sb("att_sum", [P, P])
        att_pos = sb("att_pos", [P, P])
        att_col = sb("att_col", [P, 1])
        wl_rows = sb("wl_rows", [P, P])
        wr_rows = sb("wr_rows", [P, P])
        wlT = sb("wlT", [P, P])
        wrT = sb("wrT", [P, P])
        bias_all = sb("bias_all", [P, P])
        eps_col = sb("eps_col", [P, 1])
        we1 = sb("we1", [EC, P])
        we2 = sb("we2", [P, P])
        wt_col = sb("wt_col", [P, 1])
        wn1a = sb("wn1a", [P, P])
        wn1b = sb("wn1b", [P, P])
        wn2 = sb("wn2", [P, P])
        cols = sb("cols", [P, 5])
        gate_cols = sb("gate_cols", [P, 2])
        work = sb("work", [P, 8, ROWS * P])
        xc = work[:, 0:4]
        yc = work[:, 4:8]
        xn = work[:, 0].rearrange("p (b s e) -> p b s e", b=2, s=2)
        hT = work[:, 1].rearrange("p (b s e) -> p b s e", b=2, s=2)
        xsum, xpos, mc, delta = (work[:, 2, k * GE:(k + 1) * GE] for k in range(4))
        dd = work[:, 3, 0:2 * GE].rearrange("p (k e) -> p k e", k=2)
        pp = work[:, 3, 2 * GE:4 * GE].rearrange("p (k e) -> p k e", k=2)
        accT = work[:, 4, 0:2 * GE].rearrange("p (k e) -> p k e", k=2)
        denT = work[:, 4, 2 * GE:4 * GE].rearrange("p (k e) -> p k e", k=2)
        px, attn = work[:, 5, 0:GE], work[:, 5, GE:2 * GE]
        gate_arg = work[:, 6, 0:2 * GE].rearrange("p (g e) -> p g e", g=2)
        gate_exp, gate = work[:, 6, 2 * GE:3 * GE], work[:, 6, 3 * GE:4 * GE]
        ew = work[:, 7].rearrange("p (g e) -> p g e", g=4)
        y_rows = [work[:, k, j * GE:(j + 1) * GE] for k in (4, 5) for j in (2, 3)]
        eT = work[0:EC, 1, 3 * GE:4 * GE]
        rows_i = sb("rows_i", [P, 4, 2, P], I32)
        rows_f = sb("rows_f", [P, 3, 2, P])
        keep_r = sb("keep_r", [P, 2, P])
        flag_r = sb("flag_r", [P, 2, 2, P], BF16)
        table = sb("table", [P, NG, 3, TILES], I32)
        gidx = sb("gidx", [P, 4, 2, TILES], I32)
        sidx = sb("sidx", [P, 4, TILES], I32)
        x1 = sb("x1", [P, NG, GE])
        xg = sb("xg", [P, 4, 2, GE])
        stat = sb("stat", [P, 2, 2 * TILES, 6])
        sums = sb("sums", [P, 2, 2 * TILES, 2])
        dmean = sb("dmean", [P, 2, 2 * TILES])
        var = sb("var", [P, 2, 2 * TILES])
        lnv = sb("lnv", [P, 2 * TILES])
        rstd = sb("rstd", [P, 2, 2 * TILES])
        nmr = sb("nmr", [P, 2, 2 * TILES])
        cap = sb("cap", [P, 4, GE], BF16)
        carry = sb("carry", [P, 1])
        rden = sb("rden", [P, TILES * H])
        ea = rows_i[:, :].rearrange("p b s (t d) -> p b (s t) d", d=EC).bitcast(F32)

        one_col = sb("one_col", [P, 1])
        disorder = sb("disorder", [P, 1], I32)
        row_space = x1[:, :, :].rearrange("p g e -> p (g e)")
        less = work[:, 1:8].rearrange("p a b -> p (a b)").bitcast(BF16)[:, 0:NT * P]
        small = work[:, 0]
        dst_col_i, dst_col = small[:, 0:NT].bitcast(I32), small[:, 256:256 + NT]
        n_less, n_same = small[:, 512:512 + NT], small[:, 768:768 + NT]
        rank = small[:, 1024:1024 + NT].bitcast(I32)
        before_in_tile, same = small[:, 1280:1280 + P], small[:, 1408:1408 + P]
        src_1, dst_1, rank_1 = (small[:, 1536 + k:1537 + k].bitcast(I32) for k in range(3))
        weight_1, attr_1 = small[:, 1539:1540], small[:, 1540:1540 + EC]

        bias_parts = sb("bias_parts", [3, GE], BF16)
        ones_3 = sb("ones_3", [3, P], BF16)

        psT = ps("psT", [P, 2, GE])
        psL = ps("psL", [P, 2, GE])
        psSA = ps("psSA", [P, 2, GE])
        psOD = ps("psOD", [P, 2, GE])
        psS, psA, psO, psD = psSA[:, 0], psSA[:, 1], psOD[:, 0], psOD[:, 1]
        ps_rows = [t[:, :, :].rearrange("p a e -> p (a e)") for t in (psT, psL, psSA, psOD)]

        block = ctx.enter_context(nc.Block())

        s_pool_go = sem("pool_goes_on")
        s_sp_go = sem("sp_goes_on")
        s_pe_go = sem("pe_goes_on")
        s_load = sem("weights_in")
        s_pad = sem("pads_set")
        s_rows = sem("edge_rows_in")
        s_const = sem("constants_set")
        s_ident = sem("ident_set")
        s_mix = sem("att_mix_set")
        s_zero = sem("carry_set")
        s_fl = sem("flags_made")
        s_same = sem("index_rows_made")
        s_flag_out = sem("flags_out")
        s_setT = sem("setup_transposed")
        s_viol = sem("disorder_steps")
        s_vsum = sem("disorder_summed")
        s_order = sem("disorder_known")
        s_far = sem("all_destinations_in")
        s_tri = sem("before_in_tile_set")
        s_rk = sem("rank_steps")
        s_rank = sem("ranks_made")
        s_tile = sem("tile_of_edges_in")
        s_spread = sem("tile_of_edges_spread")
        s_rows2 = sem("ordered_rows_in")
        s_edges = sem("edges_in_order")
        s_table = sem("table_ready")
        idx_in = sems("idx_in", 4)
        cap_in = sems("cap_in", 4)
        copied = sems("table_copied", 2)
        got = sems("rows_gathered", 4)
        parked = sems("x_parked", 4)
        s_stat = sem("stats_done")
        s_var = sem("var_done")
        s_rstd = sem("rstd_done")
        s_ln = sem("ln_done")
        s_nmr = sem("nmr_done")
        s_xn = sem("norm_done")
        s_T = sem("h_turned")
        s_hT = sem("h_copied")
        s_S = sem("products_done")
        s_xs = sem("sum_copied")
        s_A = sem("scores_done")
        s_mc = sem("max_steps")
        s_dl = sem("delta_done")
        s_dd = sem("exponents_done")
        s_pp = sem("exp_done")
        s_px = sem("weighted_done")
        s_acc = sem("sums_done")
        s_O = sem("sums_turned")
        s_rd = sem("den_steps")
        s_att = sem("attention_rows")
        s_x1 = sem("x1_done")
        idx2_in = sems("idx2_in", 4)
        chunk_in = sems("chunk_in", 4)
        s_xb = sem("chunk_biased")
        s_bias = sem("bias_steps")
        s_stat2 = sem("chunk_stats")
        s_var2 = sem("chunk_var")
        s_ln2 = sem("chunk_ln")
        s_rstd2 = sem("chunk_rstd")
        s_nmr2 = sem("chunk_nmr")
        s_n2 = sem("chunk_norm")
        s_y2 = sem("chunk_done")
        chunk_out = sems("chunk_out", 4)
        s_stage = sem("x1_staged")
        x1_out = sems("x1_scattered", 4)
        idx3_in = sems("idx3_in", 4)
        sidx3_in = sems("scatter_idx3_in", 4)
        in3 = sems("edges_in", 4)
        ew_in = sems("weights_of_edges_in", 4)
        got3 = sems("x1_gathered", 4)
        s_xb3 = sem("rows_biased")
        s_stat3 = sem("stats3")
        s_var3 = sem("var3")
        s_ln3 = sem("ln3")
        s_rstd3 = sem("rstd3")
        s_nmr3 = sem("nmr3")
        s_xn3 = sem("norm3")
        s_nd = sem("destinations_normed")
        s_y0 = sem("y0_done")
        s_T3 = sem("turned3")
        s_hT3 = sem("h2_copied")
        s_Te = sem("attributes_turned")
        s_eT = sem("attributes_copied")
        s_m1 = sem("mm_edge1")
        s_h1 = sem("h1_done")
        s_m2 = sem("mm_edge2")
        s_ef = sem("ef_done")
        s_arg = sem("gate_arguments")
        s_gexp = sem("gate_exp_done")
        s_gln = sem("gate_ln_done")
        s_gate = sem("gates_done")
        s_gt = sem("gated_done")
        s_m3 = sem("mm_node1")
        s_r = sem("r_done")
        s_m4 = sem("mm_node2")
        s_msg = sem("msg_done")
        s_sum = sem("msg_sums")
        s_O3 = sem("msg_turned")
        s_y3 = sem("y_done")
        y_out = sems("y_scattered", 4)

        N_WEIGHTS = 11 + 5 - 1
        keep_rows = keep_d.rearrange("(t e) -> t e", e=P)
        cap_rows = cap_d.rearrange("(t e) -> t e", e=P)

        def uses(r, c):
            return r + c // 4

        def pair_uses(r, c):
            return 2 * r + c // 2

        def load_rows(dma, kinds, loaded):
            for k, (a, shift) in kinds:
                lo = 1 if shift == -1 else 0
                hi = 1 if shift == 1 else 0
                if lo:
                    dma(rows_i[0:1, k, 0, 1:P], a[0:P - 1].rearrange("(a b) -> a b", a=1)).then_inc(loaded, 16)
                    dma(rows_i[1:P, k, 0, :], a[P - 1:TA * P - 1].rearrange("(a b) -> a b", b=P)).then_inc(loaded, 16)
                else:
                    dma(rows_i[:, k, 0, :], a[shift:TA * P + shift].rearrange("(a b) -> a b", b=P)).then_inc(loaded, 16)
                at = TA * P + shift
                dma(rows_i[0:FULL_B, k, 1, :], a[at:at + FULL_B * P].rearrange("(a b) -> a b", b=P)).then_inc(loaded, 16)
                at += FULL_B * P
                dma(rows_i[FULL_B:FULL_B + 1, k, 1, 0:REST - hi],
                    a[at:at + REST - hi].rearrange("(a b) -> a b", a=1)).then_inc(loaded, 16)

        kinds = list(enumerate(((dst, 0), (dst, -1), (dst, 1), (src, 0))))
        kinds_ordered = list(enumerate(((dst_o, 0), (dst_o, -1), (dst_o, 1), (src_o, 0))))
        COPIES = loop_turns(NG)
        assert E % COPIES == 0

        def is_disorder(eng):
            eng.wait_ge(s_order, 1)
            return eng.value_load(disorder[0:1, 0:1], min_val=0, max_val=E)

        def order_edges_sp(sp):
            dma = sp.dma_start
            dma(row_space[:, 0:E].bitcast(I32), dst.rearrange("(a e) -> a e", a=1).to_broadcast([P, E])).then_inc(s_far, 16)
            dma(dst_col_i[:, 0:NT - 1], dst[0:(NT - 1) * P].rearrange("(t p) -> p t", p=P),
                allow_slow_non_contiguous=True).then_inc(s_far, 16)
            dma(dst_col_i[0:REST, NT - 1:NT], dst[(NT - 1) * P:E].rearrange("(p a) -> p a", a=1)).then_inc(s_far, 16)
            sp.wait_ge(s_rank, 1)

            def tile(t, n):
                if not (known(t) and t == 0):
                    sp.wait_ge(s_spread, 16 * 4 * t)
                sp.sem_inc(s_sp_go, 1)
                at = bass.ds(t * P, n)
                dma(rank_1[0:n], rank[0:n, bass.ds(t, 1)]).then_inc(s_tile, 16)
                dma(src_1[0:n], src[at].rearrange("(p a) -> p a", a=1)).then_inc(s_tile, 16)
                dma(dst_1[0:n], dst[at].rearrange("(p a) -> p a", a=1)).then_inc(s_tile, 16)
                dma(weight_1[0:n], edge_weight[at].rearrange("(p a) -> p a", a=1)).then_inc(s_tile, 16)
                dma(attr_1[0:n], edge_attr[at, :]).then_inc(s_tile, 16)

            tile(0, P)
            with sp.Fori(1, NT - 1) as t:
                tile(t, P)
            tile(NT - 1, REST)
            sp.wait_ge(s_spread, 16 * 4 * NT)
            load_rows(dma, kinds_ordered, s_rows2)
            sp.sem_inc(s_edges, 16 * (COPIES + 1))

        def order_edges_pool(pool):
            pool.memset(before_in_tile, 1.0).then_inc(s_tri, 1)
            pool.wait_ge(s_tri, 1)
            pool.affine_select(out=before_in_tile, in_=before_in_tile, compare_op=ALU.is_ge, fill=0.0,
                               base=-1, pattern=[[-1, P]], channel_multiplier=1).then_inc(s_tri, 1)

            def tile(t, n):
                pool.wait_ge(s_tile, 16 * 5 * (t + 1))
                pool.sem_inc(s_pool_go, 1)
                for to, rows in ((src_o, src_1), (dst_o, dst_1), (weight_o, weight_1)):
                    pool.indirect_dma_start(
                        out=to.rearrange("(e a) -> e a", a=1), out_offset=bass.IndirectOffsetOnAxis(ap=rank_1[0:n], axis=0),
                        in_=rows[0:n], in_offset=None).then_inc(s_spread, 16)
                pool.indirect_dma_start(
                    out=attr_o, out_offset=bass.IndirectOffsetOnAxis(ap=rank_1[0:n], axis=0),
                    in_=attr_1[0:n], in_offset=None).then_inc(s_spread, 16)

            with pool.Fori(0, NT - 1) as t:
                tile(t, P)
            tile(NT - 1, REST)

        def order_edges_dve(dve):
            dve.wait_ge(s_far, 16 * 3)
            dve.tensor_copy(row_space[:, 0:E], row_space[:, 0:E].bitcast(I32))
            dve.memset(row_space[:, E:NT * P], float(NOWHERE))
            dve.tensor_copy(dst_col[:, 0:NT - 1], dst_col_i[:, 0:NT - 1])
            dve.tensor_copy(dst_col[0:REST, NT - 1:NT], dst_col_i[0:REST, NT - 1:NT]).then_inc(s_rk, 1)
            dve.wait_ge(s_tri, 2)

            def tile(t, n):
                here = row_space[0:n, bass.ds(t * P, P)]
                mine = dst_col[0:n, bass.ds(t, 1)]
                dve.wait_ge(s_rk, 3 * t + 1)
                dve.tensor_scalar(less[0:n], row_space[0:n, 0:NT * P], mine, None, ALU.is_lt)
                dve.scalar_tensor_tensor(out=same[0:n], in0=here, scalar=mine, in1=before_in_tile[0:n],
                                         op0=ALU.is_equal, op1=ALU.mult).then_inc(s_rk, 1)
                dve.wait_ge(s_rk, 3 * t + 2)
                dve.tensor_reduce(out=n_less[0:n, bass.ds(t, 1)], in_=less[0:n], axis=mybir.AxisListType.X, op=ALU.add)
                dve.tensor_reduce(out=n_same[0:n, bass.ds(t, 1)], in_=same[0:n], axis=mybir.AxisListType.X, op=ALU.add).then_inc(s_rk, 1)
                dve.tensor_scalar(row_space[:, bass.ds(t * P, P)], row_space[:, bass.ds(t * P, P)], -0.5, None, ALU.add).then_inc(s_rk, 1)

            with dve.Fori(0, NT - 1) as t:
                tile(t, P)
            tile(NT - 1, REST)
            dve.wait_ge(s_rk, 3 * NT + 1)
            dve.tensor_tensor(rank[:, 0:NT - 1], n_less[:, 0:NT - 1], n_same[:, 0:NT - 1], ALU.add)
            dve.tensor_tensor(rank[0:REST, NT - 1:NT], n_less[0:REST, NT - 1:NT], n_same[0:REST, NT - 1:NT], ALU.add).then_inc(s_rank, 1)
            dve.wait_ge(s_rows2, 16 * 13)

        @block.sync
        def _(sp):
            dma = sp.dma_start
            sp.wait_ge(s_pad, 4)
            load_rows(dma, kinds[:2], s_rows)
            unordered = is_disorder(sp)
            with sp.If(unordered != 0):
                order_edges_sp(sp)
            sp.wait_ge(s_fl, 3)
            for k, d in enumerate((keep_rows, cap_rows)):
                dma(d[0:TA, :], flag_r[:, k, 0, :]).then_inc(s_flag_out, 16)
                dma(d[TA:NT, :], flag_r[0:TB, k, 1, :]).then_inc(s_flag_out, 16)
            sp.wait_ge(s_table, 1)

            def copy_chunk(r, c):
                at = r * (4 * CH) + c * CH if not (known(r) and 4 * r + c == NC - 1) else N - CH
                if later(r, c, 2):
                    sp.wait_ge(copied[c % 2], 16 * pair_uses(r, c))
                if known(r) and 4 * r + c == NC - 1:
                    sp.wait_ge(copied[(c - 1) % 2], 16 * (pair_uses(r, c - 1) + 1))
                dma(x_tab[bass.ds(at, CH), :].rearrange("(p k) d -> p (k d)", p=P),
                    x[bass.ds(at, CH), :].rearrange("(p k) d -> p (k d)", p=P)).then_inc(copied[c % 2], 16)

            def phase1(r, c):
                c += 2
                if known(r) and 4 * r + c == NG:
                    park(r, c - 1)
                if live(r, c, NG):
                    b = c % 4
                    if later(r, c, 4):
                        sp.wait_ge(got[b], 16 * 2 * TILES * uses(r, c))
                    sp.sem_inc(s_sp_go, 1)
                    if later(r, c, 4):
                        dma(gidx[:, b], table[:, bass.ds(r * 4 + c, 1), 0:2].rearrange("p a k t -> p (a k) t")).then_inc(idx_in[b], 16)
                    if later(r, c, 4):
                        sp.wait_ge(s_dd, r * 4 + c - 3)
                    else:
                        sp.wait_ge(s_flag_out, 64)
                    dma(cap[:, b], cap_d[bass.ds(r * 4 * GE + c * GE, GE)].rearrange("(a e) -> a e", a=1)
                        .to_broadcast([P, GE])).then_inc(cap_in[b], 16)
                    copy_chunk(r, c)
                    park(r, c - 1)
            def park(r, c):
                if live(r, c, NG):
                    b = c % 4
                    sp.wait_ge(got[b], 16 * 2 * TILES * (uses(r, c) + 1))
                    dma(x1[:, bass.ds(r * 4 + c, 1)].rearrange("p a e -> p (a e)"), xg[:, b, 1, :]).then_inc(parked[b], 16)

            run_steps(sp, phase1, NG)

            def chunk_rows(tensor, r, c):
                at = N - CH if known(r) and 4 * r + c == NC - 1 else r * (4 * CH) + c * CH
                return tensor[bass.ds(at, CH), :].rearrange("(p k) d -> p (k d)", p=P)

            def load_scatter_rows(r, c, arrived):
                dma(sidx[:, c % 4], table[:, bass.ds(r * 4 + c, 1), 2].rearrange("p a t -> p (a t)")).then_inc(arrived[c % 4], 16)

            def load_gather_rows(r, c):
                if live(r, c, NG):
                    if later(r, c, 4):
                        sp.wait_ge(got3[c % 4], 16 * TILES * uses(r, c))
                    else:
                        sp.wait_ge(got[c % 4], 16 * 2 * TILES * ((NG - 1 - c % 4) // 4 + 1))
                    sp.sem_inc(s_sp_go, 1)
                    dma(gidx[:, c % 4], table[:, bass.ds(r * 4 + c, 1), 0:2].rearrange("p a k t -> p (a k) t")).then_inc(idx3_in[c % 4], 16)

            def load_edges(r, c):
                if live(r, c, NG):
                    b = c % 4
                    if later(r, c, 4):
                        sp.wait_ge(s_sum, r * 4 + c - 3)
                        sp.sem_inc(s_sp_go, 1)
                    dma(cap[:, b], keep_d[bass.ds(r * 4 * GE + c * GE, GE)].rearrange("(a e) -> a e", a=1)
                        .to_broadcast([P, GE])).then_inc(in3[b], 16)
                    if known(r) and 4 * r + c == NG - 1:
                        at, full = (NG - 1) * GE, (E - (NG - 1) * GE) // P
                        dma(ea[:, b, 0:full], attr_o[at:at + full * P, :].rearrange("(t p) d -> p t d", p=P)).then_inc(in3[b], 16)
                        dma(ea[0:REST, b, full], attr_o[at + full * P:E, :]).then_inc(in3[b], 16)
                    else:
                        dma(ea[:, b], attr_o[bass.ds(r * 4 * GE + c * GE, GE), :].rearrange("(t p) d -> p t d", p=P)).then_inc(in3[b], 16)

            load_scatter_rows(0, 0, idx2_in)
            load_scatter_rows(0, 1, idx2_in)

            def phase2(r, c):
                g = c + 2
                if live(r, g, NC):
                    b = g % 4
                    if later(r, g, 4):
                        sp.wait_ge(s_xb, 8 * r + 2 * g - 6)
                    else:
                        sp.wait_ge((s_T, s_S, s_x1, s_x1)[g], NG)
                    dma(xc[:, b], chunk_rows(x, r, g)).then_inc(chunk_in[b], 16)
                g = c + 4
                if live(r, g, NG) and not (known(r) and 4 * r + g < 2):
                    if later(r, g, 4):
                        sp.wait_ge(x1_out[g % 4], 16 * TILES * uses(r, g))
                        sp.sem_inc(s_sp_go, 1)
                    load_scatter_rows(r, g, idx2_in)
                if known(r) and 4 * r + c == 0:
                    with sp.If(unordered == 0):
                        dma(weight_o.rearrange("(a e) -> a e", a=COPIES), edge_weight.rearrange("(a e) -> a e", a=COPIES)).then_inc(s_edges, 16)
                if not known(r) and c == 0:
                    with sp.If(unordered == 0):
                        part = bass.ds((r - 1) * (E // COPIES), E // COPIES)
                        dma(attr_o[part, :], edge_attr[part, :]).then_inc(s_edges, 16)
                g = c - 2
                if live(r, g, NC):
                    sp.wait_ge(s_y2, 8 * r + 2 * g + 2)
                    if known(r) and 4 * r + g == NC - 1:
                        sp.wait_ge(chunk_out[(g - 1) % 4], 16 * (uses(r, g - 1) + 1))
                    dma(chunk_rows(out, r, g), yc[:, g % 4]).then_inc(chunk_out[g % 4], 16)
                if known(r) and 4 * r + c == NC - 3:
                    sp.wait_ge(s_edges, 16 * (COPIES + 1))
                    for k in range(4):
                        load_gather_rows(0, k)
                    for k in range(3):
                        load_edges(0, k)

            run_steps(sp, phase2, NG)

            def phase3(r, c):
                if not (known(r) and 4 * r + c < 0):
                    load_gather_rows(r, c + 4)
                    load_edges(r, c + 3)
                    if live(r, c, NG):
                        if later(r, c, 4):
                            sp.wait_ge(y_out[c % 4], 16 * TILES * uses(r, c))
                        else:
                            sp.wait_ge(x1_out[c % 4], 16 * TILES * ((NG - 1 - c % 4) // 4 + 1))
                        sp.sem_inc(s_sp_go, 1)
                        load_scatter_rows(r, c, sidx3_in)
                        load_weights(r, c + 3)

            def load_weights(r, c):
                if live(r, c, NG):
                    b = c % 4
                    if later(r, c, 4):
                        sp.wait_ge(s_arg, r * 4 + c - 3)
                        sp.sem_inc(s_sp_go, 1)
                    n = E - (NG - 1) * GE if known(r) and 4 * r + c == NG - 1 else GE
                    dma(ew[:, b, 0:n], weight_o[bass.ds(r * 4 * GE + c * GE, n)].rearrange("(a e) -> a e", a=1)
                        .to_broadcast([P, n])).then_inc(ew_in[b], 16)

            sp.wait_ge(chunk_out[3], 16 * ((NC - 1 - 3) // 4 + 1))
            for k in range(3):
                load_weights(0, k)
            run_steps(sp, phase3, NG)
            for b in range(2):
                sp.wait_ge(copied[b], 16 * ((NC - 1 - b) // 2 + 1))
            for b in range(4):
                sp.wait_ge(chunk_out[b], 16 * ((NC - 1 - b) // 4 + 1))
                sp.wait_ge(x1_out[b], 16 * TILES * ((NG - 1 - b) // 4 + 1))
                sp.wait_ge(y_out[b], 16 * TILES * ((NG - 1 - b) // 4 + 1))

        def arrived3(r, c):
            per = 16 * 2
            return per * (uses(r, c) + 1) + (16 if known(r) and 4 * r + c == NG - 1 else 0)

        @block.gpsimd
        def _(pool):
            for k, v in enumerate((-1, -1, -1, 0)):
                pool.memset(rows_i[:, k], v).then_inc(s_pad, 1)
            pool.memset(ident[:, :], 0.0).then_inc(s_const, 1)
            pool.memset(att_pos[:, :], 1.0).then_inc(s_const, 1)
            pool.wait_ge(s_const, 2)
            pool.affine_select(out=ident[:, :], in_=ident[:, :], compare_op=ALU.not_equal, fill=1.0,
                               base=0, pattern=[[-1, P]], channel_multiplier=1).then_inc(s_ident, 1)
            heads = att_pos[:, :].rearrange("p (h c) -> p h c", c=C)
            pool.affine_select(out=heads, in_=heads, compare_op=ALU.is_ge, fill=0.0,
                               base=0, pattern=[[-C, H], [0, C]], channel_multiplier=1).then_inc(s_mix, 1)
            pool.wait_ge(s_mix, 1)
            pool.affine_select(out=heads, in_=heads, compare_op=ALU.is_ge, fill=0.0,
                               base=C - 1, pattern=[[C, H], [0, C]], channel_multiplier=-1).then_inc(s_mix, 1)

            with pool.If(is_disorder(pool) != 0):
                order_edges_pool(pool)

            def phase1(r, c):
                c += 2
                if live(r, c, NG):
                    b = c % 4
                    if later(r, c, 4):
                        pool.wait_ge(idx_in[b], 16 * uses(r, c))
                        pool.wait_ge(s_xn, r * 4 + c - 3)
                        pool.wait_ge(parked[b], 16 * uses(r, c))
                    pool.sem_inc(s_pool_go, 1)
                    rows = gidx[:, b] if later(r, c, 4) else table[:, c, 0:2]
                    for j in range(TILES):
                        for side in range(2):
                            pool.indirect_dma_start(
                                out=xg[:, b, side, j * P:(j + 1) * P], out_offset=None, in_=x,
                                in_offset=bass.IndirectOffsetOnAxis(ap=rows[:, side, j:j + 1], axis=0)
                            ).then_inc(got[b], 16)

            pool.wait_ge(s_table, 1)
            run_steps(pool, phase1, NG)

            for b in range(2):
                pool.wait_ge(copied[b], 16 * ((NC - 1 - b) // 2 + 1))

            def phase2(r, c):
                c += 2
                if live(r, c, NG):
                    b = c % 4
                    pool.wait_ge(idx2_in[b], 16 * (uses(r, c) + 1))
                    pool.wait_ge(s_stage, r * 4 + c + 1)
                    pool.sem_inc(s_pool_go, 1)
                    for j in range(TILES):
                        pool.indirect_dma_start(
                            out=x_tab, out_offset=bass.IndirectOffsetOnAxis(ap=sidx[:, b, j:j + 1], axis=0),
                            in_=xg[:, b, 1, j * P:(j + 1) * P], in_offset=None,
                            bounds_check=N - 1, oob_is_err=False).then_inc(x1_out[b], 16)

            run_steps(pool, phase2, NG)

            for b in range(4):
                pool.wait_ge(x1_out[b], 16 * TILES * ((NG - 1 - b) // 4 + 1))

            def gather_x1(r, g):
                if live(r, g, NG):
                    b = g % 4
                    pool.wait_ge(idx3_in[b], 16 * (uses(r, g) + 1))
                    if later(r, g, 4):
                        pool.wait_ge(s_xn3, r * 4 + g - 3)
                    pool.sem_inc(s_pool_go, 1)
                    for j in range(TILES):
                        pool.indirect_dma_start(
                            out=xg[:, b, 0, j * P:(j + 1) * P], out_offset=None, in_=x_tab,
                            in_offset=bass.IndirectOffsetOnAxis(ap=gidx[:, b, 0, j:j + 1], axis=0)
                        ).then_inc(got3[b], 16)

            def phase3(r, c):
                gather_x1(r, c + 3)
                g = c - 2
                if live(r, g, NG):
                    b = g % 4
                    if known(r) and 4 * r + g == 0:
                        for k in range(4):
                            pool.wait_ge(chunk_out[k], 16 * ((NC - 1 - k) // 4 + 1))
                    pool.wait_ge(sidx3_in[b], 16 * (uses(r, g) + 1))
                    pool.wait_ge(s_y3, r * 4 + g + 1)
                    pool.sem_inc(s_pool_go, 1)
                    for j in range(TILES):
                        pool.indirect_dma_start(
                            out=out, out_offset=bass.IndirectOffsetOnAxis(ap=sidx[:, b, j:j + 1], axis=0),
                            in_=y_rows[b][:, j * P:(j + 1) * P], in_offset=None,
                            bounds_check=N - 1, oob_is_err=False).then_inc(y_out[b], 16)

            gather_x1(0, 0)
            run_steps(pool, phase3, NG)

        def stats_rows(dve, rows, n, b, s_stats):
            for j in range(n):
                last = dve.bn_stats(stat[:, b, j, :], rows(j))
            last.then_inc(s_stats, 1)

        def stats_means(dve, n, b, s_stats, g):
            dve.wait_ge(s_stats, 3 * g + 1)
            dve.tensor_tensor(dmean[:, b, 0:n], stat[:, b, 0:n, 1], stat[:, b, 0:n, 4], ALU.subtract)
            dve.tensor_tensor(sums[:, b, 0:n, :], stat[:, b, 0:n, 1:3], stat[:, b, 0:n, 4:6], ALU.add).then_inc(s_stats, 1)

        def stats_square(dve, n, b, s_stats, g):
            dve.wait_ge(s_stats, 3 * g + 2)
            dve.tensor_tensor(dmean[:, b, 0:n], dmean[:, b, 0:n], dmean[:, b, 0:n], ALU.mult).then_inc(s_stats, 1)

        def stats_var(dve, n, b, s_stats, s_variance, g):
            dve.wait_ge(s_stats, 3 * g + 3)
            dve.scalar_tensor_tensor(out=var[:, b, 0:n], in0=dmean[:, b, 0:n], scalar=P / 4.0, in1=sums[:, b, 0:n, 1],
                                     op0=ALU.mult, op1=ALU.add).then_inc(s_variance, 1)

        def negative_mean(dve, n, b):
            return dve.scalar_tensor_tensor(out=nmr[:, b, 0:n], in0=sums[:, b, 0:n, 0], scalar=-0.5,
                                            in1=rstd[:, b, 0:n], op0=ALU.mult, op1=ALU.mult)

        @block.vector
        def _(dve):
            dve.memset(eps_col[:, :], EPS)
            dve.memset(one_col[:, :], 1.0)
            dve.memset(carry[:, :], 0.0).then_inc(s_zero, 1)
            dve.wait_ge(s_rows, 16 * 13)
            dve.tensor_tensor(rows_f[:, 0], rows_i[:, 1], rows_i[:, 0], ALU.is_gt).then_inc(s_viol, 1)
            dve.wait_ge(s_viol, 1)
            dve.tensor_reduce(out=dmean[:, 0, 0:1], in_=rows_f[:, 0].rearrange("p a b -> p (a b)"),
                              axis=mybir.AxisListType.X, op=ALU.add).then_inc(s_viol, 1)
            dve.wait_ge(s_vsum, 1)
            dve.tensor_copy(disorder[0:1, :], psA[0:1, 0:1]).then_inc(s_order, 1)
            with dve.If(is_disorder(dve) != 0):
                order_edges_dve(dve)
            dve.tensor_tensor(rows_f[:, 2], rows_i[:, 0], rows_i[:, 2], ALU.is_equal).then_inc(s_same, 1)
            dve.tensor_copy(rows_f[:, 0], rows_i[:, 3])
            dve.tensor_scalar(rows_f[:, 1], rows_i[:, 0], 0.0, None, ALU.max)
            dve.wait_ge(s_same, 1)
            dve.scalar_tensor_tensor(out=rows_f[:, 2], in0=rows_f[:, 2], scalar=float(NOWHERE), in1=rows_i[:, 0],
                                     op0=ALU.mult, op1=ALU.add).then_inc(s_same, 1)
            dve.tensor_tensor(keep_r[:, :, :], rows_i[:, 0], rows_i[:, 1], ALU.is_equal).then_inc(s_fl, 1)
            dve.wait_ge(s_fl, 1)
            dve.tensor_copy(flag_r[:, 0], keep_r[:, :, :]).then_inc(s_fl, 1)
            dve.tensor_scalar(flag_r[:, 1], keep_r[:, :, :], 2 * BIG, -BIG, ALU.mult, ALU.add).then_inc(s_fl, 1)
            dve.wait_ge(s_setT, 1)
            turned = psT[:, :, :].rearrange("p a (k t) -> p (a k) t", t=P)
            for k in range(3):
                dve.tensor_copy(table[:, 0:TA // TILES, k, :],
                                turned[:, k, :].rearrange("p (g t) -> p g t", t=TILES))
            dve.wait_ge(s_setT, 2)
            turned = psL[:, :, :].rearrange("p a (k t) -> p (a k) t", t=P)
            for k in range(3):
                last = dve.tensor_copy(table[:, TA // TILES:NG, k, :],
                                       turned[:, k, 0:TB].rearrange("p (g t) -> p g t", t=TILES))
            last.then_inc(s_table, 1)
            dve.wait_ge(s_setT, 3)
            dve.tensor_copy(wlT[:, :], psS[:, 0:P])
            dve.tensor_copy(wrT[:, :], psS[:, P:2 * P])
            dve.wait_ge(s_load, 16 * N_WEIGHTS)
            dve.wait_ge(s_mix, 2)
            dve.wait_ge(s_zero, 1)
            dve.tensor_scalar(att_sum[:, :], att_pos[:, :], att_col[:, 0:1], NEG_SLOPE, ALU.mult, ALU.mult).then_inc(s_zero, 1)
            dve.wait_ge(s_zero, 2)
            dve.tensor_scalar(att_pos[:, :], att_pos[:, :], att_col[:, 0:1], 1 - NEG_SLOPE, ALU.mult, ALU.mult)
            dve.tensor_scalar(gate_cols[:, 0:1], cols[:, 2:3], -1.0, None, ALU.mult)
            dve.tensor_scalar(gate_cols[:, 1:2], cols[:, 2:3], -1.0, LEAST, ALU.mult, ALU.add).then_inc(s_table, 1)
            part = [work[0:3, 7, k * P:(k + 1) * P] for k in range(6)]
            rounded = [flag_r[0:3, 0, 0, :], flag_r[0:3, 0, 1, :]]
            dve.wait_ge(s_flag_out, 64)
            dve.memset(ones_3[:, :], 1.0)
            dve.tensor_copy(rounded[0], bias_all[0:3, :]).then_inc(s_bias, 1)
            dve.wait_ge(s_bias, 1)
            dve.tensor_copy(part[0], rounded[0]).then_inc(s_bias, 1)
            dve.wait_ge(s_bias, 2)
            dve.tensor_tensor(part[1], bias_all[0:3, :], part[0], ALU.subtract).then_inc(s_bias, 1)
            dve.wait_ge(s_bias, 3)
            dve.tensor_copy(rounded[1], part[1]).then_inc(s_bias, 1)
            dve.wait_ge(s_bias, 4)
            dve.tensor_copy(part[2], rounded[1]).then_inc(s_bias, 1)
            dve.wait_ge(s_bias, 5)
            dve.tensor_tensor(part[3], part[1], part[2], ALU.subtract)
            dve.tensor_scalar(part[4], part[0], ident[0:3, 0:1], None, ALU.mult).then_inc(s_bias, 1)
            dve.wait_ge(s_bias, 6)
            dve.scalar_tensor_tensor(out=part[5], in0=part[2], scalar=ident[0:3, 1:2], in1=part[4],
                                     op0=ALU.mult, op1=ALU.add).then_inc(s_bias, 1)
            dve.wait_ge(s_bias, 7)
            dve.scalar_tensor_tensor(out=part[4], in0=part[3], scalar=ident[0:3, 2:3], in1=part[5],
                                     op0=ALU.mult, op1=ALU.add).then_inc(s_bias, 1)
            dve.wait_ge(s_bias, 8)
            for k in range(TILES):
                last = dve.tensor_copy(bias_parts[:, k * P:(k + 1) * P], part[4])
            last.then_inc(s_bias, 1)

            def phase1(r, c):
                g, b, h = r * 4 + c, c % 4, c % 2
                now, norm, before = live(r, c, NG), live(r, c + 2, NG), live(r, c - 1, NG)
                n, bn, bp = 2 * TILES, (c + 2) % 4, (c - 1) % 4
                if norm:
                    dve.wait_ge(got[bn], 16 * n * (uses(r, c + 2) + 1))
                    stats_rows(dve, lambda j: xg[:, bn, j // TILES, (j % TILES) * P:(j % TILES + 1) * P], n, h, s_stat)
                if now:
                    dve.wait_ge(cap_in[b], 16 * (uses(r, c) + 1))
                    dve.tensor_tensor(mc[:, 0:1], carry[:, :], cap[:, b, 0:1], ALU.min).then_inc(s_mc, 1)
                if norm:
                    stats_means(dve, n, h, s_stat, g + 2)
                if now:
                    dve.wait_ge(s_A, g + 1)
                    dve.wait_ge(s_mc, 3 * g + 1)
                    dve.tensor_tensor_scan(mc[:, 1:GE], psA[:, 0:GE - 1], cap[:, b, 1:GE], mc[:, 0:1],
                                           ALU.max, ALU.min).then_inc(s_mc, 1)
                if norm:
                    stats_square(dve, n, h, s_stat, g + 2)
                if now:
                    dve.wait_ge(s_mc, 3 * g + 2)
                    dve.tensor_tensor(delta[:, :], psA[:, :], mc[:, :], ALU.subtract).then_inc(s_dl, 1)
                if norm:
                    stats_var(dve, n, h, s_stat, s_var, g + 2)
                if now:
                    dve.tensor_tensor(carry[:, :], psA[:, GE - 1:GE], mc[:, GE - 1:GE], ALU.max).then_inc(s_mc, 1)
                    dve.wait_ge(s_dl, g + 1)
                    dve.tensor_scalar(dd[:, 0, :], delta[:, :], 0.0, -1.0, ALU.max, ALU.mult)
                    dve.tensor_scalar(dd[:, 1, :], delta[:, :], 0.0, None, ALU.min).then_inc(s_dd, 1)
                if norm:
                    dve.wait_ge(s_rstd, g + 3)
                    if later(r, c + 2, 2):
                        dve.wait_ge(s_xn, g + 1)
                    negative_mean(dve, n, h).then_inc(s_nmr, 1)
                if before:
                    dve.wait_ge(s_O, g)
                    dve.tensor_scalar(rden[:, :], psD[:, 0:GE:C], 1e-16, None, ALU.add).then_inc(s_rd, 1)
                if before:
                    dve.wait_ge(s_rd, 2 * g - 1)
                    dve.reciprocal(rden[:, :], rden[:, :]).then_inc(s_rd, 1)
                    dve.wait_ge(s_rd, 2 * g)
                    dve.tensor_tensor(attn[:, :].rearrange("p (k c) -> p k c", c=C),
                                      psO[:, :].rearrange("p (k c) -> p k c", c=C),
                                      rden[:, :].unsqueeze(2).to_broadcast([P, TILES * H, C]), ALU.mult).then_inc(s_att, 1)
                first = known(r) and r * 4 + c == 0
                if now:
                    dve.wait_ge(s_pp, g + 1)
                    dve.tensor_tensor(px[:, :], pp[:, 1, :], psL[:, h, :], ALU.mult).then_inc(s_px, 1)
                if before:
                    dve.wait_ge(parked[bp], 16 * (uses(r, c - 1) + 1))
                    dve.wait_ge(s_att, g)
                    row = x1[:, bass.ds(g - 1, 1)].rearrange("p a e -> p (a e)")
                    dve.tensor_tensor(row, attn[:, :], row, ALU.add).then_inc(s_x1, 1)
                if now:
                    if later(r, c, 2):
                        dve.wait_ge(s_O, g - 1)
                    if later(r, c, 1):
                        dve.wait_ge(s_acc, 2 * g)
                    dve.wait_ge(s_px, g + 1)
                    dve.tensor_tensor_scan(accT[:, h, :], pp[:, 0, :], px[:, :],
                                           0.0 if first else accT[:, 1 - h, GE - 1:GE], ALU.mult, ALU.add).then_inc(s_acc, 1)
                    dve.tensor_tensor_scan(denT[:, h, :], pp[:, 0, :], pp[:, 1, :],
                                           0.0 if first else denT[:, 1 - h, GE - 1:GE], ALU.mult, ALU.add).then_inc(s_acc, 1)

            run_steps(dve, phase1, NG)

            HALF = ROWS // 2

            def phase2(r, c):
                for f in range(2):
                    m = 8 * r + 2 * c + f
                    now, before = live(r, c, NC), live(r, c - 1, NC)
                    if now:
                        slot = ps_rows[2 * (c % 2) + f].rearrange("p (k d) -> p k d", d=D)
                        dve.wait_ge(s_xb, m + 1)
                        for j in range(HALF):
                            if j == 3 and not (known(r) and 4 * r + c == 0 and f == 0):
                                dve.wait_ge(s_rstd2, m)
                                negative_mean(dve, HALF, 1 - f).then_inc(s_nmr2, 1)
                            last = dve.bn_stats(stat[:, f, j, :], slot[:, j, :])
                        last.then_inc(s_stat2, 1)
                    elif f == 0 and before:
                        dve.wait_ge(s_rstd2, m)
                        negative_mean(dve, HALF, 1 - f).then_inc(s_nmr2, 1)
                    if before:
                        o, cut = (c - 1) % 4, slice(f * HALF * P, (f + 1) * HALF * P)
                        dve.wait_ge(s_n2, m - 1)
                        dve.tensor_tensor(yc[:, o, cut], yc[:, o, cut], ps_rows[2 * ((c - 1) % 2) + f], ALU.add).then_inc(s_y2, 1)
                    if now:
                        stats_means(dve, HALF, f, s_stat2, m)
                        stats_square(dve, HALF, f, s_stat2, m)
                        stats_var(dve, HALF, f, s_stat2, s_var2, m)

            run_steps(dve, phase2, NC)

            def phase3(r, c):
                g = r * 4 + c
                now, norm, after, before = live(r, c, NG), live(r, c + 2, NG), live(r, c + 1, NG), live(r, c - 1, NG)
                h, b, bn, ba, bp = c % 2, c % 4, (c + 2) % 4, (c + 1) % 4, (c - 1) % 4
                n = 2 * TILES
                bias_rows = bias_all[:, :].unsqueeze(1).to_broadcast([P, TILES, D])
                if norm:
                    dve.wait_ge(got3[bn], 16 * TILES * (uses(r, c + 2) + 1))
                    src_rows = xg[:, bn, 0, :].rearrange("p (k d) -> p k d", d=D)
                    dve.tensor_tensor(src_rows, src_rows, bias_rows, ALU.add).then_inc(s_xb3, 1)
                if after:
                    dve.wait_ge(s_rstd3, g + 2)
                    if later(r, c + 1, 2):
                        dve.wait_ge(s_xn3, g)
                    negative_mean(dve, n, 1 - h).then_inc(s_nmr3, 1)
                if norm:
                    if later(r, c + 2, 4):
                        dve.wait_ge(s_y3, g - 1)
                    dst_rows = xg[:, bn, 1, :].rearrange("p (k d) -> p k d", d=D)
                    dve.tensor_tensor(dst_rows, x1[:, bass.ds(g + 2, 1)].rearrange("p a (k d) -> p (a k) d", d=D), bias_rows, ALU.add).then_inc(s_xb3, 1)
                if after:
                    dve.wait_ge(s_nmr3, g + 2)
                    for k in range(TILES):
                        j, part = TILES + k, slice(k * P, (k + 1) * P)
                        last = dve.tensor_scalar(xn[:, 0, 1, part], xg[:, ba, 1, part], rstd[:, 1 - h, j:j + 1], nmr[:, 1 - h, j:j + 1],
                                                 ALU.mult, ALU.add)
                    last.then_inc(s_nd, 1)
                if before:
                    dve.wait_ge(s_y0, g)
                    dve.wait_ge(s_O3, g)
                    if later(r, c - 1, 4):
                        dve.wait_ge(y_out[bp], 16 * TILES * uses(r, c - 1))
                    dve.tensor_tensor(y_rows[bp], psO[:, :], xg[:, bp, 1, :], ALU.add).then_inc(s_y3, 1)
                if after:
                    dve.wait_ge(s_nd, g + 2)
                    dve.scalar_tensor_tensor(out=xg[:, ba, 1, :], in0=xn[:, 0, 1, :], scalar=0.0, in1=xg[:, ba, 1, :],
                                             op0=ALU.max, op1=ALU.add).then_inc(s_y0, 1)
                if norm:
                    dve.wait_ge(s_xb3, 2 * (g + 3))
                    stats_rows(dve, lambda j: xg[:, bn, j // TILES, (j % TILES) * P:(j % TILES + 1) * P], n, h, s_stat3)
                if after:
                    dve.wait_ge(s_ef, g + 2)
                    dve.wait_ge(s_gate, g + 2)
                    if later(r, c + 1, 1):
                        dve.wait_ge(s_m3, g + 1)
                    dve.tensor_tensor(delta[:, :], gate, pp[:, 1, :], ALU.mult).then_inc(s_gt, 1)
                if norm:
                    stats_means(dve, n, h, s_stat3, g + 2)
                    if known(r) and 4 * r + c < -1:
                        dve.wait_ge(chunk_out[2], 16 * ((NC - 3) // 4 + 1))
                    dve.wait_ge(ew_in[bn], 16 * (uses(r, c + 2) + 1))
                    if later(r, c + 2, 2):
                        dve.wait_ge(s_gexp, g + 1)
                    dve.tensor_scalar(gate_arg[:, h, :], ew[:, bn, :], wt_col[:, 0:1], gate_cols[:, 1:2], ALU.mult, ALU.max).then_inc(s_arg, 1)
                if now:
                    if known(r) and 4 * r + c == 0:
                        for k in range(2):
                            dve.wait_ge(chunk_out[k], 16 * ((NC - 1 - k) // 4 + 1))
                    dve.wait_ge(in3[b], arrived3(r, c))
                    dve.wait_ge(s_msg, g + 1)
                    if later(r, c, 1):
                        dve.wait_ge(s_sum, g)
                    if later(r, c, 2):
                        dve.wait_ge(s_O3, g - 1)
                    first = known(r) and r * 4 + c == 0
                    dve.tensor_tensor_scan(accT[:, h, :], cap[:, b, :], px[:, :],
                                           0.0 if first else accT[:, 1 - h, GE - 1:GE], ALU.mult, ALU.add).then_inc(s_sum, 1)
                if norm:
                    stats_square(dve, n, h, s_stat3, g + 2)
                    stats_var(dve, n, h, s_stat3, s_var3, g + 2)

            run_steps(dve, phase3, NG)

        def make_scales(act, n, b, s_variance, s_log, s_scale, g):
            act.wait_ge(s_variance, g + 1)
            act.activation(lnv[:, 0:n], var[:, b, 0:n], ACT.Ln, scale=1.0 / P, bias=eps_col[:, 0:1]).then_inc(s_log, 1)
            act.wait_ge(s_log, g + 1)
            act.activation(rstd[:, b, 0:n], lnv[:, 0:n], ACT.Exp, scale=-0.5).then_inc(s_scale, 1)

        def normalise(act, rows_in, rows_out, blocks, b):
            for j in blocks:
                last = act.activation(rows_out(j), rows_in(j), ACT.Relu, scale=rstd[:, b, j:j + 1], bias=nmr[:, b, j:j + 1])
            return last

        @block.scalar
        def _(act):
            act.preload_act_table_set("natural_log_exp_and_others")
            act.wait_ge(s_pad, 4)
            load_rows(act.dma_start, kinds[2:], s_rows)
            for tile, source in ((wl_rows, W_l), (wr_rows, W_r), (we1, We1), (we2, We2),
                                 (wt_col, Wt.rearrange("a d -> d a")), (wn1a, Wn1[0:P, :]), (wn1b, Wn1[P:2 * P, :]), (wn2, Wn2),
                                 (att_col, att.rearrange("h (c a) -> (h c) a", a=1)),
                                 (bias_all, bias0.rearrange("(a d) -> a d", a=1).to_broadcast([P, P]))):
                act.dma_start(tile[:, :], source).then_inc(s_load, 16)
            for k, source in enumerate((be1, be2, bt, bn1, bn2)):
                act.dma_start(cols[:, k:k + 1], source.rearrange("(d a) -> d a", a=1)).then_inc(s_load, 16)
            act.wait_ge(s_table, 2)

            def phase1(r, c):
                g, h = r * 4 + c, c % 2
                norm, b = live(r, c + 2, NG), (c + 2) % 4
                rows_in = lambda j: xg[:, b, j // TILES, (j % TILES) * P:(j % TILES + 1) * P]
                rows_out = lambda j: xn[:, h, j // TILES, (j % TILES) * P:(j % TILES + 1) * P]
                if live(r, c + 1, NG):
                    act.wait_ge(s_T, g + 2)
                    if later(r, c + 1, 2):
                        act.wait_ge(s_S, g)
                    act.copy(hT[:, 1 - h], psT[:, :, :]).then_inc(s_hT, 1)
                if norm:
                    make_scales(act, 2 * TILES, h, s_var, s_ln, s_rstd, g + 2)
                if live(r, c, NG):
                    act.wait_ge(s_dd, g + 1)
                    act.activation(pp[:, :, :], dd[:, :, :], ACT.Exp).then_inc(s_pp, 1)
                if norm:
                    act.wait_ge(s_nmr, g + 3)
                    if later(r, c + 2, 2):
                        act.wait_ge(s_T, g + 1)
                    normalise(act, rows_in, rows_out, range(TILES), h)
                if live(r, c + 1, NG):
                    act.wait_ge(s_S, g + 2)
                    if later(r, c + 1, 1):
                        act.wait_ge(s_A, g + 1)
                    act.copy(xsum[:, :], psS[:, :])
                    act.activation(xpos[:, :], psS[:, :], ACT.Relu).then_inc(s_xs, 1)
                if norm:
                    normalise(act, rows_in, rows_out, range(TILES, 2 * TILES), h).then_inc(s_xn, 1)

            run_steps(act, phase1, NG)

            act.wait_ge(s_x1, NG)

            def phase2(r, c):
                g, h = r * 4 + c, c % 2
                for f in range(2):
                    if live(r, c, NC):
                        b, m, n = c % 4, 8 * r + 2 * c + f, ROWS // 2
                        make_scales(act, n, f, s_var2, s_ln2, s_rstd2, m)
                    if f == 0 and live(r, c + 2, NG):
                        bs = (c + 2) % 4
                        if later(r, c + 2, 4):
                            act.wait_ge(x1_out[bs], 16 * TILES * uses(r, c + 2))
                        act.copy(xg[:, bs, 1, :], x1[:, bass.ds(g + 2, 1)].rearrange("p a e -> p (a e)")).then_inc(s_stage, 1)
                    if live(r, c, NC):
                        act.wait_ge(s_nmr2, m + 1)
                        if f == 0 and later(r, c, 4):
                            act.wait_ge(chunk_out[b], 16 * uses(r, c))
                        rows = ps_rows[2 * h + f].rearrange("p (k d) -> p k d", d=D)
                        normed = yc[:, b, f * n * P:(f + 1) * n * P].rearrange("p (k d) -> p k d", d=D)
                        normalise(act, lambda j: rows[:, j, :], lambda j: normed[:, j, :], range(n), f).then_inc(s_n2, 1)

            run_steps(act, phase2, NG)
            act.wait_ge(s_y2, 2 * NC)
            for b in (1, 2):
                act.wait_ge(chunk_out[b], 16 * ((NC - 1 - b) // 4 + 1))

            def phase3(r, c):
                g, h = r * 4 + c, c % 2
                now, after, b = live(r, c, NG), live(r, c + 1, NG), (c + 1) % 4
                rows_in = lambda j: xg[:, b, j // TILES, (j % TILES) * P:(j % TILES + 1) * P]
                rows_out = lambda j: xn[:, 1 - h, j // TILES, (j % TILES) * P:(j % TILES + 1) * P]
                if after:
                    act.wait_ge(s_Te, g + 2)
                    if later(r, c + 1, 1):
                        act.wait_ge(s_m1, g + 1)
                    act.copy(eT[:, :], psT[0:EC, 1, :]).then_inc(s_eT, 1)
                if now:
                    act.wait_ge(s_T3, g + 1)
                    if later(r, c, 1):
                        act.wait_ge(s_m3, g)
                    act.copy(hT[:, 0, 0, :], psT[:, 0, :]).then_inc(s_hT3, 1)
                if after:
                    make_scales(act, 2 * TILES, 1 - h, s_var3, s_ln3, s_rstd3, g + 1)
                    act.wait_ge(s_arg, g + 2)
                    act.activation(gate_exp, gate_arg[:, 1 - h, :], ACT.Exp, scale=-1.0, bias=gate_cols[:, 0:1]).then_inc(s_gexp, 1)
                    act.wait_ge(s_nmr3, g + 2)
                    if later(r, c + 1, 2):
                        act.wait_ge(s_T3, g)
                    normalise(act, rows_in, rows_out, range(TILES), 1 - h).then_inc(s_xn3, 1)
                if after:
                    act.wait_ge(s_m1, g + 2)
                    act.activation(dd[:, 0, :], psS[:, :], ACT.Relu, bias=cols[:, 0:1]).then_inc(s_h1, 1)
                    act.wait_ge(s_gexp, g + 2)
                    act.activation(gate_exp, gate_exp, ACT.Ln, bias=one_col[:, 0:1]).then_inc(s_gln, 1)
                if now:
                    act.wait_ge(s_m3, g + 1)
                    act.activation(dd[:, 1, :], psL[:, 1, :], ACT.Relu, bias=cols[:, 3:4]).then_inc(s_r, 1)
                if after:
                    act.wait_ge(s_gln, g + 2)
                    if later(r, c + 1, 1):
                        act.wait_ge(s_gt, g + 1)
                    act.activation(gate, gate_exp, ACT.Exp, scale=-1.0).then_inc(s_gate, 1)
                    act.wait_ge(s_m2, g + 2)
                    if later(r, c + 1, 1):
                        act.wait_ge(s_gt, g + 1)
                    act.activation(pp[:, 1, :], psA[:, :], ACT.Identity, bias=cols[:, 1:2]).then_inc(s_ef, 1)
                if now:
                    act.wait_ge(s_m4, g + 1)
                    if later(r, c, 1):
                        act.wait_ge(s_sum, g)
                    act.activation(px[:, :], psD[:, :], ACT.Identity, bias=cols[:, 4:5]).then_inc(s_msg, 1)

            run_steps(act, phase3, NG)

        @block.tensor
        def _(pe):
            pe.wait_ge(s_viol, 2)
            pe.matmul(psA[0:1, 0:1], dmean[:, 0, 0:1], one_col[:, :], start=True, stop=True).then_inc(s_vsum, 1)
            pe.wait_ge(s_ident, 1)
            pe.wait_ge(s_same, 2)
            for half_, n, to in ((0, TA, psT), (1, TB, psL)):
                for k in range(3):
                    last = pe.transpose(to[:, k // TILES, k * P:k * P + n], rows_f[0:n, k, half_, :], ident[0:n, 0:n])
                last.then_inc(s_setT, 1)
            pe.wait_ge(s_load, 16 * N_WEIGHTS)
            pe.transpose(psS[:, 0:P], wl_rows[:, :], ident[:, :])
            pe.transpose(psS[:, P:2 * P], wr_rows[:, :], ident[:, :]).then_inc(s_setT, 1)
            pe.wait_ge(s_table, 2)

            def phase1(r, c):
                g, h = r * 4 + c, c % 2
                if live(r, c + 1, NG):
                    pe.wait_ge(s_xn, g + 2)
                    if later(r, c + 1, 1):
                        pe.wait_ge(s_hT, g + 1)
                    for side in range(2):
                        for j in range(TILES):
                            last = pe.transpose(psT[:, side, j * P:(j + 1) * P], xn[:, 1 - h, side, j * P:(j + 1) * P], ident[:, :])
                    last.then_inc(s_T, 1)
                if live(r, c - 1, NG):
                    pe.wait_ge(s_acc, 2 * g)
                    if later(r, c - 1, 1):
                        pe.wait_ge(s_att, g - 1)
                    for j in range(TILES):
                        pe.transpose(psD[:, j * P:(j + 1) * P], denT[:, 1 - h, j * P:(j + 1) * P], ident[:, :])
                    for j in range(TILES):
                        last = pe.transpose(psO[:, j * P:(j + 1) * P], accT[:, 1 - h, j * P:(j + 1) * P], ident[:, :])
                    last.then_inc(s_O, 1)
                if live(r, c + 1, NG):
                    pe.wait_ge(s_hT, g + 2)
                    if later(r, c + 1, 2):
                        pe.wait_ge(s_px, g)
                    if later(r, c + 1, 1):
                        pe.wait_ge(s_xs, g + 1)
                    pe.matmul(psS[:, :], wlT[:, :], hT[:, 1 - h, 0, :], start=True, stop=False)
                    pe.matmul(psS[:, :], wrT[:, :], hT[:, 1 - h, 1, :], start=False, stop=True)
                    pe.matmul(psL[:, 1 - h, :], wlT[:, :], hT[:, 1 - h, 0, :], start=True, stop=True).then_inc(s_S, 1)
                    pe.wait_ge(s_xs, g + 2)
                    if later(r, c + 1, 1):
                        pe.wait_ge(s_dd, g + 1)
                    pe.matmul(psA[:, :], att_sum[:, :], xsum[:, :], start=True, stop=False)
                    pe.matmul(psA[:, :], att_pos[:, :], xpos[:, :], start=False, stop=True).then_inc(s_A, 1)

            run_steps(pe, phase1, NG)

            def phase2(r, c):
                for f in range(2):
                    if live(r, c, NC):
                        m, b, h = 8 * r + 2 * c + f, c % 4, c % 2
                        slot = ps_rows[2 * h + f]
                        if known(r) and 4 * r + c < 2:
                            pe.wait_ge((s_hT, s_px, s_dd, s_x1)[m], NG)
                        else:
                            pe.wait_ge(s_y2, m - 3)
                        if f == 0:
                            pe.wait_ge(chunk_in[b], 16 * (uses(r, c) + 1))
                        for j in range(2):
                            to = slot[:, j * GE:(j + 1) * GE]
                            at = (2 * f + j) * GE
                            pe.matmul(to, ones_3[:, :], bias_parts[:, :], start=True, stop=False)
                            last = pe.matmul(to, ident[:, :], xc[:, b, at:at + GE], start=False, stop=True)
                        last.then_inc(s_xb, 1)

            pe.wait_ge(s_bias, 9)
            run_steps(pe, phase2, NC)
            pe.wait_ge(s_y2, 2 * NC)

            def phase3(r, c):
                g, h = r * 4 + c, c % 2
                now, after, norm = live(r, c, NG), live(r, c + 1, NG), live(r, c + 2, NG)
                if live(r, c - 1, NG):
                    pe.wait_ge(s_sum, g)
                    if later(r, c - 1, 1):
                        pe.wait_ge(s_y3, g - 1)
                    for j in range(TILES):
                        last = pe.transpose(psO[:, j * P:(j + 1) * P], accT[:, 1 - h, j * P:(j + 1) * P], ident[:, :])
                    last.then_inc(s_O3, 1)
                if after:
                    pe.wait_ge(s_eT, g + 2)
                    if later(r, c + 1, 1):
                        pe.wait_ge(s_h1, g + 1)
                    pe.matmul(psS[:, :], we1[:, :], eT[:, :], start=True, stop=True).then_inc(s_m1, 1)
                if now:
                    pe.wait_ge(s_hT3, g + 1)
                    pe.wait_ge(s_gt, g + 1)
                    if later(r, c, 1):
                        pe.wait_ge(s_r, g)
                    pe.matmul(psL[:, 1, :], wn1a[:, :], hT[:, 0, 0, :], start=True, stop=False)
                    pe.matmul(psL[:, 1, :], wn1b[:, :], delta[:, :], start=False, stop=True).then_inc(s_m3, 1)
                if after:
                    pe.wait_ge(s_xn3, g + 2)
                    if later(r, c + 1, 1):
                        pe.wait_ge(s_hT3, g + 1)
                    for j in range(TILES):
                        last = pe.transpose(psT[:, 0, j * P:(j + 1) * P], xn[:, 1 - h, 0, j * P:(j + 1) * P], ident[:, :])
                    last.then_inc(s_T3, 1)
                    pe.wait_ge(s_h1, g + 2)
                    if later(r, c + 1, 1):
                        pe.wait_ge(s_ef, g + 1)
                    pe.matmul(psA[:, :], we2[:, :], dd[:, 0, :], start=True, stop=True).then_inc(s_m2, 1)
                if now:
                    pe.wait_ge(s_r, g + 1)
                    if later(r, c, 1):
                        pe.wait_ge(s_msg, g)
                    pe.matmul(psD[:, :], wn2[:, :], dd[:, 1, :], start=True, stop=True).then_inc(s_m4, 1)
                if norm:
                    b = (c + 2) % 4
                    pe.wait_ge(in3[b], arrived3(r, c + 2))
                    if later(r, c + 2, 1):
                        pe.wait_ge(s_eT, g + 2)
                    pe.sem_inc(s_pe_go, 1)
                    for j in range(TILES):
                        last = pe.transpose(psT[0:EC, 1, j * P:(j + 1) * P], ea[:, b, j, :], ident[:, :])
                    last.then_inc(s_Te, 1)

            run_steps(pe, phase3, NG)


_INS = ['x', 'src', 'dst', 'edge_attr_64', 'edge_weight', 'L0_gnn_W_l', 'L0_gnn_W_r', 'L0_gnn_att', 'L0_gnn_bias',
        'L1_gnn_We1', 'L1_gnn_be1', 'L1_gnn_We2', 'L1_gnn_be2', 'L1_gnn_Wt', 'L1_gnn_bt',
        'L1_gnn_Wn1', 'L1_gnn_bn1', 'L1_gnn_Wn2', 'L1_gnn_bn2']


def kernel(**inputs):
    import numpy as _np
    import concourse.bacc as _bacc
    from concourse.bass_utils import run_bass_kernel_spmd as _run

    nc = _bacc.Bacc("TRN2", target_bir_lowering=False, num_devices=1)
    arrays, args = {}, []
    for name in _INS:
        a = _np.ascontiguousarray(inputs[name])
        arrays[f"in_{name}"] = a
        args.append(nc.dram_tensor(f"in_{name}", a.shape, mybir.dt.from_np(a.dtype), kind="ExternalInput").ap())
    out = nc.dram_tensor("out_0", arrays["in_x"].shape, F32, kind="ExternalOutput").ap()
    gnn_program(nc, *args, out)
    r = _run(nc, [arrays], core_ids=[0])
    return r.results[0]["out_0"]
```
